# Optimizing a Trainium2 kernel written in Bass

```python
import numpy as np
import jax
import jax.numpy as jnp

def _softmax(x, axis=-1):
    return jax.nn.softmax(x, axis=axis)

def _gelu(x):
    return jax.nn.gelu(x, approximate=True)

def _silu(x):
    return jax.nn.silu(x)

def _sigmoid(x):
    return jax.nn.sigmoid(x)

def _layernorm(x, axis=-1, eps=1e-05):
    m = jnp.mean(x, axis=axis, keepdims=True)
    v = jnp.var(x, axis=axis, keepdims=True)
    return (x - m) / jnp.sqrt(v + eps)

def _scatter_add(tgt, idx, src, axis=0):
    return tgt.at[idx].add(src)

def _segment_sum(src, seg, n):
    return jax.ops.segment_sum(src, seg, n)
kernel_name = 'mk_adaln_d1_jaxref_r8_0cb672'

def setup_inputs(seed: int=0):
    np.random.seed(seed)
    _w = jnp.asarray

    def _L0_attn_setup():
        import jax, jax.numpy as jnp
        import numpy as np
        HEADS = 8
        BLOCK = 32
        key = jax.random.key(seed)
        ks = jax.random.split(key, 4)
        b, n, d, f = (4, 512, 128, 128)
        x = jax.random.normal(ks[0], (b, n, d), dtype=jnp.float32)
        w_qkv = jax.random.normal(ks[1], (3 * d, d), dtype=jnp.float32) * d ** (-0.5)
        w_out = jax.random.normal(ks[2], (d, d), dtype=jnp.float32) * d ** (-0.5)
        b_out = jnp.zeros((d,), dtype=jnp.float32)
        proj = jax.random.normal(ks[3], (HEADS, d // HEADS, f), dtype=jnp.float32) * (d // HEADS) ** (-0.5)
        return {'x': x, 'w_qkv': w_qkv, 'w_out': w_out, 'b_out': b_out, 'proj': proj}
    _L0_attn_in = _L0_attn_setup()

    def _L0_ffn_setup():
        import jax, jax.numpy as jnp
        import numpy as np
        E, D, F, GATE_DIM = (8, 128, 512, 16)
        B, T = (2, 256)
        key = jax.random.key(seed)
        ks = jax.random.split(key, 7)
        s = 0.02
        return {'hidden_states': jax.random.normal(ks[0], (B, T, D), dtype=jnp.float32), 'w_red': jax.random.normal(ks[1], (D, GATE_DIM), dtype=jnp.float32) * s, 'wg': jax.random.normal(ks[2], (E, GATE_DIM), dtype=jnp.float32), 'w1': jax.random.normal(ks[3], (E, D, F), dtype=jnp.float32) * s, 'b1': jax.random.normal(ks[4], (E, F), dtype=jnp.float32) * s, 'w2': jax.random.normal(ks[5], (E, F, D), dtype=jnp.float32) * s, 'b2': jax.random.normal(ks[6], (E, D), dtype=jnp.float32) * s}
    _L0_ffn_in = _L0_ffn_setup()
    _L0_c = _w((lambda *s: np.random.randn(*s).astype(np.float32) * 0.05)(4, 128))
    _L0_wmod = _w((lambda *s: np.random.randn(*s).astype(np.float32) * 0.05)(128, 6 * 128) * 128 ** (-0.5))
    _d = {'L0_attn_x': _L0_attn_in['x'], 'L0_attn_w_qkv': _L0_attn_in['w_qkv'], 'L0_attn_w_out': _L0_attn_in['w_out'], 'L0_attn_b_out': _L0_attn_in['b_out'], 'L0_attn_proj': _L0_attn_in['proj'], 'L0_ffn_w_red': _L0_ffn_in['w_red'], 'L0_ffn_wg': _L0_ffn_in['wg'], 'L0_ffn_w1': _L0_ffn_in['w1'], 'L0_ffn_b1': _L0_ffn_in['b1'], 'L0_ffn_w2': _L0_ffn_in['w2'], 'L0_ffn_b2': _L0_ffn_in['b2'], 'L0_c': _L0_c, 'L0_wmod': _L0_wmod}
    _x0 = _d['L0_attn_x']
    _d['L0_attn_x'] = jax.random.normal(jax.random.fold_in(jax.random.key(seed), 1), (4, 1024, 128), dtype=_x0.dtype)
    del _x0
    return _d

def reference(L0_attn_x, L0_attn_w_qkv, L0_attn_w_out, L0_attn_b_out, L0_attn_proj, L0_ffn_w_red, L0_ffn_wg, L0_ffn_w1, L0_ffn_b1, L0_ffn_w2, L0_ffn_b2, L0_c, L0_wmod):

    def _L0_attn_ref(x, w_qkv, w_out, b_out, proj):
        import jax, jax.numpy as jnp
        import numpy as np
        HEADS = 8
        BLOCK = 32
        b, n, d = x.shape
        h = HEADS
        hd = d // h
        nb = n // BLOCK
        qkv = x @ w_qkv.T
        q, k, v = jnp.split(qkv, 3, axis=-1)

        def to_blocks(t):
            return t.reshape(b, n, h, hd).transpose(0, 2, 1, 3).reshape(b, h, nb, BLOCK, hd)
        q, k, v = (to_blocks(q), to_blocks(k), to_blocks(v))
        qp = jax.nn.elu(jnp.einsum('bhcsd,hdf->bhcsf', q, proj)) + 1.0
        kp = jax.nn.elu(jnp.einsum('bhcsd,hdf->bhcsf', k, proj)) + 1.0
        kv = jnp.einsum('bhcsf,bhcsd->bhcfd', kp, v)
        num = jnp.einsum('bhcsf,bhcfd->bhcsd', qp, kv)
        ksum = kp.sum(axis=3)
        z = 1.0 / (jnp.einsum('bhcsf,bhcf->bhcs', qp, ksum) + 1e-08)
        out = num * z[..., None]
        out = out.reshape(b, h, n, hd).transpose(0, 2, 1, 3).reshape(b, n, d)
        return out @ w_out.T + b_out

    def _L0_ffn_ref(hidden_states, w_red, wg, w1, b1, w2, b2):
        import jax, jax.numpy as jnp
        import numpy as np
        E, D, F, GATE_DIM = (8, 128, 512, 16)
        B, T = (2, 256)
        b, t, c = hidden_states.shape
        x = hidden_states.reshape(-1, c)
        red = x @ w_red
        wg_n = wg / jnp.maximum(jnp.linalg.norm(wg, axis=1, keepdims=True), 0.0001)
        logits = red @ wg_n.T
        gates = jax.nn.softmax(logits, axis=1)
        idx = jnp.argmax(gates, axis=1)
        scores = jnp.take_along_axis(gates, idx[:, None], axis=1)
        h = jax.nn.gelu(jnp.einsum('td,edf->etf', x, w1) + b1[:, None, :], approximate=False)
        y = jnp.einsum('etf,efd->etd', h, w2) + b2[:, None, :]
        out = jnp.take_along_axis(y, idx[None, :, None], axis=0)[0]
        out = out * scores
        return out.reshape(b, t, c)
    x = L0_attn_x
    mod = (_silu(L0_c) @ L0_wmod).reshape(L0_c.shape[0], 6, 1, -1)
    sa, ca, ga, sb, cb, gb = (mod[:, 0], mod[:, 1], mod[:, 2], mod[:, 3], mod[:, 4], mod[:, 5])
    ga = (2 * (ga >= 0) - 1) * jnp.maximum(jnp.abs(ga), 0.25)
    gb = (2 * (gb >= 0) - 1) * jnp.maximum(jnp.abs(gb), 0.25)
    h = _layernorm(x, axis=-1) * (1 + ca) + sa
    x = x + ga * _L0_attn_ref(h, L0_attn_w_qkv, L0_attn_w_out, L0_attn_b_out, L0_attn_proj)
    h = _layernorm(x, axis=-1) * (1 + cb) + sb
    x = x + gb * _L0_ffn_ref(h, L0_ffn_w_red, L0_ffn_wg, L0_ffn_w1, L0_ffn_b1, L0_ffn_w2, L0_ffn_b2)
    return x

_drawn_inputs = setup_inputs


def setup_inputs(seed=0):
    import zlib

    import numpy as np

    out = dict(_drawn_inputs(seed))
    spreads = {'L0_attn_b_out': (0.0, 0.341)}
    factors = {'L0_attn_proj': 8.0,
     'L0_ffn_w_red': 8.0,
     'L0_ffn_wg': 8.0,
     'L0_ffn_w1': 8.0,
     'L0_ffn_b1': 8.0,
     'L0_ffn_w2': 8.0,
     'L0_ffn_b2': 23.641}
    for name, (base, spread) in spreads.items():
        noise = np.random.default_rng([zlib.crc32(name.encode()), seed]).standard_normal(out[name].shape)
        drawn = base * np.exp(spread * noise) if base else spread * noise
        out[name] = jnp.asarray(drawn.astype(out[name].dtype))
    for name, factor in factors.items():
        out[name] = (out[name] * factor).astype(out[name].dtype)
    return out
```

```python
from contextlib import ExitStack

import concourse.bass as bass
from concourse import mybir

P = 128
ALU = mybir.AluOpType
ACT = mybir.ActivationFunctionType
AX = mybir.AxisListType
F32 = mybir.dt.float32
BF16 = mybir.dt.bfloat16
I32 = mybir.dt.int32

EPS = 1e-5


def adaln_kernel(nc, x, w_qkv, w_out, b_out, proj, w_red, wg, w1, b1, w2, b2, c_cols, wmod, out):
    B, N, D = x.shape
    H, HD, FEAT = proj.shape
    E, _, F = w1.shape
    GD = w_red.shape[1]
    T = B * N
    NT = T // P
    TG = 4
    GT = TG * P
    NG = T // GT
    GB_ = N // GT
    BLK = 32
    NC = P // BLK
    VW = HD + 1
    HH = H // 2
    FC = F // P
    REGION = T + P
    DUMMY = E * REGION
    SLOTS = NT + E - 1
    R = 3 * D + 1
    assert D == P and FEAT == P and H * HD == P and HH == NC and 2 * HD == BLK

    xf = x.rearrange("b n d -> (b n) d")
    of = out.rearrange("b n d -> (b n) d")
    sorted_rows = nc.dram_tensor("sorted_rows", [DUMMY + P, R], F32, kind="Internal").ap()

    ctx = ExitStack()
    with ctx:
        def sb(name, shape, dt=F32):
            return ctx.enter_context(nc.sbuf_tensor(name, shape, dt))

        def sem(name):
            return ctx.enter_context(nc.semaphore(name))

        x_all = sb("x_all", [P, NT, D])
        wqkv_sb = sb("wqkv_sb", [P, 3, D])
        proj_bd = sb("proj_bd", [P, H, FEAT])
        mix = sb("mix", [P, 2, H, FEAT])
        wvT = sb("wvT", [P, P])
        wo_sb = sb("wo_sb", [P, P])
        wo_perm = sb("wo_perm", [P, P])
        woT = sb("woT", [P, P])
        wo_g = sb("wo_g", [P, NG, P])
        bout_bc = sb("bout_bc", [P, D])
        wmod_sb = sb("wmod_sb", [P, 6 * D])
        cT = sb("cT", [P, B])
        ecT = sb("ecT", [P, B])
        siluT = sb("siluT", [P, B])
        silu_bc = sb("silu_bc", [P, B, P])
        modT = sb("modT", [P, 2, NG])
        mod_bc = sb("mod_bc", [P, NG, 4, D])
        wred_sb = sb("wred_sb", [P, GD])
        wredT = sb("wredT", [GD, P])
        wg_sb = sb("wg_sb", [E, GD])
        wg_sq = sb("wg_sq", [E, GD])
        wg_n = sb("wg_n", [E, 4])
        wg_u = sb("wg_u", [E, GD])
        wgT = sb("wgT", [GD, E])
        w_gate = sb("w_gate", [P, E])
        w1_sb = sb("w1_sb", [P, E * F])
        w2_sb = sb("w2_sb", [P, E * FC * D])
        b1_bc = sb("b1_bc", [P, E * F])
        b2_bc = sb("b2_bc", [P, E * D])
        ident = sb("ident", [P, P])
        before = sb("before", [P, P], BF16)
        ones_b = sb("ones_b", [P, P], BF16)
        blk_mask = sb("blk_mask", [P, NC, VW])
        rev = sb("rev", [P, E])
        ids = sb("ids", [P, NT])
        pad_rec = sb("pad_rec", [P, R])

        ln1_st = sb("ln1_st", [P, TG, 6])
        ln1_mv = sb("ln1_mv", [P, TG, 2])
        ln1_ve = sb("ln1_ve", [P, TG])
        ln2_ve = sb("ln2_ve", [P, TG])
        neg_half = sb("neg_half", [P, TG])
        ln1_rs = sb("ln1_rs", [P, TG])
        xn = sb("xn", [P, TG, D])
        hT = sb("hT", [P, GT])
        ebuf = sb("ebuf", [P, 2, 2, GT])
        phi = sb("phi", [P, 4, 2, GT])
        a_sb = sb("a_sb", [P, 2, HH, TG, BLK])
        vbd = sb("vbd", [P, TG, H, NC, VW])
        den = sb("den", [P, TG * NC])
        rden = sb("rden", [P, TG * NC])
        o_sb = sb("o_sb", [P, TG * NC, 2, HD])
        oT = sb("oT", [P, TG, P])
        x2 = sb("x2", [P, TG, D])
        ln2_st = sb("ln2_st", [P, TG, 6])
        ln2_mv = sb("ln2_mv", [P, TG, 2])
        ln2_rs = sb("ln2_rs", [P, TG])
        h2 = sb("h2", [P, TG, D])
        h2m = sb("h2m", [P, TG, D])
        h2T = sb("h2T", [P, TG, P])
        top = sb("top", [P, TG])
        lgd = sb("lgd", [P, TG, E])
        lge = sb("lge", [P, TG, E])
        lgs = sb("lgs", [P, TG])
        score = sb("score", [P, TG])
        cand = sb("cand", [P, TG, E])
        cmax = sb("cmax", [P, TG])
        pick = sb("pick", [P, TG, E], BF16)
        carry = sb("carry", [P, E])
        pref = sb("pref", [P, TG, E])
        posf = sb("posf", [P, TG, E])
        posr = sb("posr", [P, TG])
        pos = sb("pos", [P, TG], I32)
        rec = sb("rec", [P, TG, R])

        cnt = sb("cnt", [P, E])
        full = sb("full", [P, E, NT])
        nt = sb("nt", [P, E])
        endt = sb("endt", [P, 2, E])
        skip = sb("skip", [P, E])
        past = sb("past", [P, SLOTS, E])
        hop = sb("hop", [P, SLOTS, E])
        expf = sb("expf", [P, 2, SLOTS])
        rowf = sb("rowf", [P, 2, SLOTS])
        region0 = sb("region0", [P, E])
        tiles128 = sb("tiles128", [P, NT])
        slot_no = sb("slot_no", [P, SLOTS])
        exp_i = sb("exp_i", [P, SLOTS], I32)
        row_i = sb("row_i", [P, SLOTS], I32)
        carry_i = sb("carry_i", [P, E], I32)

        rin = sb("rin", [P, 2, R])
        sT = sb("sT", [P, 2, P])
        hb = sb("hb", [P, 2, F])
        gT = sb("gT", [P, 2, FC, P])
        y1 = sb("y1", [P, 2, D])
        y2 = sb("y2", [P, 2, D])
        yo = sb("yo", [P, 2, D])
        tok = sb("tok", [P, 2], I32)

        ps = ctx.enter_context(nc.psum_tensor("ps", [P, 8, 512], F32))
        x_ps = [ps[:, 2 * i:2 * i + 2, :] for i in range(2)]
        a_ps = [ps[:, 4 + i, 0:GT // NC] for i in range(2)]
        o_ps = ps[:, 6, 0:TG * NC * VW]
        m_ps = ps[:, 7, :]

        l_attn = sem("l_attn"); l_mod = sem("l_mod"); l_gate = sem("l_gate"); l_x0 = sem("l_x0"); l_x = sem("l_x")
        l_exp = sem("l_exp"); l_pad = sem("l_pad")
        c_pool = sem("c_pool"); c_dve = sem("c_dve"); p_set = sem("p_set"); set_dve = sem("set_dve"); set_act = sem("set_act")
        set_pool = sem("set_pool")
        s_x = sem("s_x"); s_a = sem("s_a"); s_av = sem("s_av"); s_y = sem("s_y"); s_xt = sem("s_xt")
        s_v = sem("s_v"); s_h2t = sem("s_h2t"); s_lg = sem("s_lg"); s_rk = sem("s_rk")
        s_exp = sem("s_exp"); s_asb = sem("s_asb"); s_ht = sem("s_ht"); s_h2ts = sem("s_h2ts"); s_ex = sem("s_ex")
        s_neg = sem("s_neg"); s_xb = sem("s_xb"); s_rec = sem("s_rec"); s_gbs = sem("s_gbs"); s_scat = sem("s_scat")
        s_phi = sem("s_phi"); s_ln1 = sem("s_ln1"); s_xn = sem("s_xn"); s_vbd = sem("s_vbd"); s_nrm = sem("s_nrm")
        s_on = sem("s_on"); s_ot = sem("s_ot"); s_x2 = sem("s_x2"); s_ln2 = sem("s_ln2"); s_h2 = sem("s_h2")
        s_rt = sem("s_rt"); s_pick = sem("s_pick"); s_sc = sem("s_sc"); s_lgd = sem("s_lgd"); s_ps = sem("s_ps"); s_pos = sem("s_pos")
        s_nh = sem("s_nh"); s_gs = sem("s_gs"); s_pr = sem("s_pr"); f_s = sem("f_s"); seq_pool = sem("seq_pool"); seq_dve = sem("seq_dve"); s_rs1 = sem("s_rs1"); s_rs2 = sem("s_rs2"); s_tab = sem("s_tab"); s_table = sem("s_table"); s_tail = sem("s_tail")
        f_in = [sem("f_in0"), sem("f_in1")]
        f_t = sem("f_t"); f_ts = sem("f_ts"); f_h = sem("f_h"); f_hb = sem("f_hb"); f_ht = sem("f_ht"); f_g = sem("f_g")
        f_y = sem("f_y"); f_yd = sem("f_yd"); f_tok = sem("f_tok"); f_done = sem("f_done")
        f_out = [sem("f_out0"), sem("f_out1")]

        block = ctx.enter_context(nc.Block())

        @block.sync
        def _(sp):
            sp.dma_start(wqkv_sb[:, :, :], w_qkv.rearrange("(j r) d -> r j d", j=3)).then_inc(l_attn, 16)
            sp.dma_start(proj_bd[:, 0, :], proj.rearrange("h k f -> (h k) f")).then_inc(l_attn, 16)
            sp.dma_start(cT[:, :], c_cols).then_inc(l_mod, 16)
            sp.dma_start(wmod_sb[:, :], wmod).then_inc(l_mod, 16)
            xt = xf.rearrange("(t p) d -> p t d", p=P)
            sp.dma_start(x_all[:, 0:TG, :], xt[:, 0:TG, :]).then_inc(l_x0, 16)
            sp.dma_start(wo_sb[:, :], w_out).then_inc(l_gate, 16)
            sp.dma_start(bout_bc[:, :], b_out.rearrange("(a d) -> a d", a=1).partition_broadcast(P)).then_inc(l_gate, 16)
            sp.dma_start(wred_sb[:, :], w_red).then_inc(l_gate, 16)
            sp.dma_start(wg_sb[:, :], wg).then_inc(l_gate, 16)
            sp.dma_start(x_all[:, TG:NT, :], xt[:, TG:NT, :]).then_inc(l_x, 16)
            sp.dma_start(w1_sb[:, :].rearrange("p (e f) -> p e f", e=E), w1.rearrange("e d f -> d e f")).then_inc(l_exp, 16)
            sp.dma_start(w2_sb[:, :].rearrange("p (e c d) -> p e c d", e=E, c=FC),
                         w2.rearrange("e (c p) d -> p e c d", p=P)).then_inc(l_exp, 16)
            sp.dma_start(b1_bc[:, :], b1.rearrange("(a e) f -> a (e f)", a=1).partition_broadcast(P)).then_inc(l_exp, 16)
            sp.dma_start(b2_bc[:, :], b2.rearrange("(a e) f -> a (e f)", a=1).partition_broadcast(P)).then_inc(l_exp, 16)
            sp.wait_ge(c_dve, 1)
            sp.dma_start(sorted_rows[DUMMY:DUMMY + P, :], pad_rec[:, :]).then_inc(s_tail, 16)
            sp.wait_ge(s_table, 1)
            for e in range(E):
                row = sp.value_load(carry_i[0:1, e:e + 1], min_val=e * REGION, max_val=e * REGION + T)
                sp.dma_start(sorted_rows[bass.ds(row, P), :], pad_rec[:, :]).then_inc(s_tail, 16)
            sp.wait_ge(s_tail, 16 * (E + 1))
            sp.wait_ge(s_scat, 16 * NT)
            sp.wait_ge(s_table, 2)

            def load_slot(s, b, k):
                row = sp.value_load(row_i[0:1, bass.ds(s, 1)], min_val=0, max_val=DUMMY)
                sp.dma_start(rin[:, b, :], sorted_rows[bass.ds(row, P), :]).then_inc(f_in[b], 16)

            load_slot(0, 0, 0)
            load_slot(1, 1, 0)
            with sp.Fori(2, SLOTS - 1, 2) as s:
                for b in range(2):
                    sp.wait_ge(f_done, s + b - 1)
                    load_slot(s + b, b, None)
            sp.wait_ge(f_done, SLOTS - 2)
            load_slot(SLOTS - 1, (SLOTS - 1) % 2, None)

        @block.gpsimd
        def _(pool):
            g_ = nc.gpsimd
            g_.memset(ident[:, :], 0.0).then_inc(c_pool, 1)
            g_.memset(ones_b[:, :], 1.0).then_inc(c_pool, 1)
            g_.memset(blk_mask[:, :, :], 1.0).then_inc(c_pool, 1)
            g_.memset(neg_half[:, :], -0.5)
            g_.iota(tiles128[:, :], [[P, NT]], base=0, channel_multiplier=0, allow_small_or_imprecise_dtypes=True)
            g_.iota(region0[:, :], [[REGION, E]], base=0, channel_multiplier=0, allow_small_or_imprecise_dtypes=True)
            g_.iota(slot_no[:, :], [[1, SLOTS]], base=0, channel_multiplier=0, allow_small_or_imprecise_dtypes=True)
            g_.iota(rev[:, :], [[-1, E]], base=E, channel_multiplier=0, allow_small_or_imprecise_dtypes=True)
            g_.iota(ids[:, :], [[P, NT]], base=0, channel_multiplier=1,
                    allow_small_or_imprecise_dtypes=True).then_inc(c_pool, 1)
            pool.wait_ge(c_pool, 4)
            g_.affine_select(out=ident[:, :], in_=ident[:, :], compare_op=ALU.not_equal, fill=1.0,
                             base=0, pattern=[[-1, P]], channel_multiplier=1).then_inc(c_pool, 1)
            g_.affine_select(out=before[:, :], in_=ones_b[:, :], compare_op=ALU.is_gt, fill=0.0,
                             base=0, pattern=[[1, P]], channel_multiplier=-1).then_inc(c_pool, 1)
            g_.affine_select(out=blk_mask[:, :, :], in_=blk_mask[:, :, :], compare_op=ALU.is_ge, fill=0.0,
                             base=0, pattern=[[-BLK, NC], [0, VW]], channel_multiplier=1).then_inc(c_pool, 1)
            pool.wait_ge(c_pool, 7)
            g_.affine_select(out=blk_mask[:, :, :], in_=blk_mask[:, :, :], compare_op=ALU.is_ge, fill=0.0,
                             base=BLK - 1, pattern=[[BLK, NC], [0, VW]], channel_multiplier=-1).then_inc(c_pool, 1)
            pool.wait_ge(l_attn, 32)
            g_.affine_select(out=proj_bd[:, 1:H, :], in_=proj_bd[:, 0:1, :].broadcast_to([P, H - 1, FEAT]),
                             compare_op=ALU.is_ge, fill=0.0, base=-HD,
                             pattern=[[-HD, H - 1], [0, FEAT]], channel_multiplier=1).then_inc(c_pool, 1)
            pool.wait_ge(c_pool, 9)
            g_.affine_select(out=proj_bd[:, :, :], in_=proj_bd[:, :, :], compare_op=ALU.is_ge, fill=0.0,
                             base=HD - 1, pattern=[[HD, H], [0, FEAT]], channel_multiplier=-1).then_inc(c_pool, 1)

            def rsqrt(out, in_, done):
                n = in_.shape[0]
                g_.tensor_tensor(out, in_, neg_half[0:n, 0:in_.shape[1]], ALU.pow).then_inc(done, 1)

            pool.wait_ge(s_ln1, 3)
            rsqrt(ln1_rs[:, :], ln1_ve[:, :], s_rs1)
            pool.wait_ge(c_dve, 7)
            rsqrt(wg_n[:, 2:3], wg_n[:, 1:2], set_pool)
            pool.wait_ge(set_dve, 6)
            g_.tensor_tensor(wo_g[:, :, :], woT[:, :].unsqueeze(1).broadcast_to([P, NG, P]), mod_bc[:, :, 0, :],
                             ALU.mult).then_inc(set_pool, 1)
            pool.wait_ge(set_pool, 2)
            g_.tensor_tensor(mod_bc[:, :, 0, :], mod_bc[:, :, 0, :],
                             bout_bc[:, :].unsqueeze(1).broadcast_to([P, NG, D]), ALU.mult).then_inc(set_pool, 1)

            def wait_then(s, value):
                pool.wait_ge(s, value)
                pool.sem_inc(seq_pool, 1)

            def residual_base(g):
                pool.wait_ge(l_x, 16)
                pool.wait_ge(l_x0, 16)
                pool.wait_ge(set_pool, 3)
                g_.tensor_tensor(x2[:, :, :], x_all[:, bass.ds(g * TG, TG), :],
                                 mod_bc[:, bass.ds(g, 1), 0, :].broadcast_to([P, TG, D]), ALU.add).then_inc(s_xb, 1)

            def build_records(g, first):
                pool.wait_ge(s_h2, g + 1)
                if not first:
                    wait_then(s_scat, 16 * TG * g)
                g_.tensor_copy(rec[:, :, 0:D], h2m[:, :, :])
                g_.tensor_copy(rec[:, :, D:2 * D], x2[:, :, :])
                g_.tensor_copy(rec[:, :, 3 * D:3 * D + 1], ids[:, bass.ds(g * TG, TG)].unsqueeze(2)).then_inc(s_rec, 1)

            def build_scale(g):
                pool.wait_ge(s_sc, g + 1)
                g_.tensor_tensor(rec[:, :, 2 * D:3 * D], mod_bc[:, bass.ds(g, 1), 3, :].broadcast_to([P, TG, D]),
                                 score[:, :].unsqueeze(2).broadcast_to([P, TG, D]), ALU.mult).then_inc(s_gbs, 1)

            def scatter(g):
                pool.wait_ge(s_pos, g + 1)
                pool.wait_ge(s_gbs, g + 1)
                wait_then(s_rec, g + 1)
                for t in range(TG):
                    g_.indirect_dma_start(out=sorted_rows[:, :],
                                          out_offset=bass.IndirectOffsetOnAxis(ap=pos[:, t:t + 1], axis=0),
                                          in_=rec[:, t, :], in_offset=None).then_inc(s_scat, 16)

            def step(g, now, prev, prev2, first2=False, nxt=True):
                for h in range(H):
                    if h == 0 and nxt:
                        pool.wait_ge(s_ln1, 3 * g + 6)
                        rsqrt(ln1_rs[:, :], ln1_ve[:, :], s_rs1)
                    if h == 5 and prev:
                        pool.wait_ge(s_ln2, 3 * g)
                        rsqrt(ln2_rs[:, :], ln2_ve[:, :], s_rs2)
                    if h == 1 and prev2:
                        build_records(g - 2, first2)
                    if h == 3 and prev:
                        if prev2:
                            pool.wait_ge(s_rec, g - 1)
                        residual_base(g - 1)
                    if h == 5 and prev2:
                        build_scale(g - 2)
                    if h == 7 and prev2:
                        scatter(g - 2)

            step(0, True, False, False)
            step(1, True, True, False)
            step(2, True, True, True, first2=True)
            with pool.Fori(3, NG - 1) as g:
                step(g, True, True, True)
            step(NG - 1, True, True, True, nxt=False)
            step(NG, False, True, True, nxt=False)
            step(NG + 1, False, False, True, nxt=False)

            def put(s, b):
                wait_then(f_yd, s + 1)
                g_.indirect_dma_start(out=of[:, :], out_offset=bass.IndirectOffsetOnAxis(ap=tok[:, b:b + 1], axis=0),
                                      in_=yo[:, b, :], in_offset=None, bounds_check=T - 1,
                                      oob_is_err=False).then_inc(f_out[b], 16)

            with pool.Fori(0, SLOTS - 1, 2) as s:
                put(s, 0)
                put(s + 1, 1)
            put(SLOTS - 1, 0)
            pool.wait_ge(f_out[0], 16 * ((SLOTS + 1) // 2))
            pool.wait_ge(f_out[1], 16 * (SLOTS // 2))

        @block.scalar
        def _(act):
            act.wait_ge(l_mod, 32)
            nc.scalar.activation(ecT[:, :], cT[:, :], ACT.Exp, scale=-1.0).then_inc(set_act, 1)
            act.wait_ge(p_set, 1)
            for j in range(2):
                nc.scalar.copy(mix[:, 1, 4 * j:4 * j + 4, :].rearrange("p h f -> p (h f)"), ps[:, 2 + j, :]).then_inc(set_act, 1)

            def exp_head(g, h):
                act.wait_ge(s_x, H * g + h + 1)
                if not (isinstance(g, int) and g == 0 and h < 2):
                    act.wait_ge(s_phi, H * g + h - 1)
                nc.scalar.activation(ebuf[:, h % 2, :, :], x_ps[h % 2], ACT.Relu, scale=-1.0).then_inc(s_neg, 1)
                act.wait_ge(s_neg, H * g + h + 1)
                nc.scalar.activation(ebuf[:, h % 2, :, :], ebuf[:, h % 2, :, :], ACT.Exp, scale=-1.0).then_inc(s_exp, 1)

            def keep_a(g, h, first):
                act.wait_ge(s_a, H * g + h + 1)
                if h % HH == 0 and not first:
                    act.wait_ge(s_av, 2 * g + h // HH - 1)
                nc.scalar.copy(a_sb[:, h // HH, h % HH, :, :], a_ps[h % 2].rearrange("p (t s) -> p t s", t=TG)).then_inc(s_asb, 1)

            def keep_hT(g, first):
                act.wait_ge(s_xt, g + 1)
                if first:
                    act.wait_ge(set_dve, 2)
                else:
                    act.wait_ge(s_x, H * g)
                nc.scalar.activation(hT[:, :], m_ps, ACT.Identity, bias=modT[:, 0, bass.ds(g, 1)],
                                     scale=modT[:, 1, bass.ds(g, 1)]).then_inc(s_ht, 1)

            def keep_h2T(g):
                act.wait_ge(s_h2t, g + 1)
                nc.scalar.copy(h2T[:, :, :].rearrange("p t d -> p (t d)"), m_ps).then_inc(s_h2ts, 1)

            def gate_exp(g):
                act.wait_ge(s_lgd, g + 1)
                nc.scalar.activation(lge[:, :, :], lgd[:, :, :], ACT.Exp).then_inc(s_ex, 1)

            def step(g, now, prev, prev2, nxt, first=False, first2=False):
                for h in range(H):
                    if h == 0 and prev2:
                        keep_h2T(g - 2)
                    if now:
                        exp_head(g, h)
                    if h == 3 and prev2:
                        gate_exp(g - 2)
                    if h < 2 and prev:
                        keep_a(g - 1, h + 6, first2)
                    if h >= 2 and now:
                        keep_a(g, h - 2, first)
                if nxt:
                    keep_hT(g + 1, False)

            keep_hT(0, True)
            step(0, True, False, False, True, first=True)
            step(1, True, True, False, True, first2=True)
            with act.Fori(2, NG - 1) as g:
                step(g, True, True, True, True)
            step(NG - 1, True, True, True, False)
            step(NG, False, True, True, False)
            step(NG + 1, False, False, True, False)

            def keep_sT(s, b):
                act.wait_ge(f_t, s + 1)
                nc.scalar.copy(sT[:, b, :], ps[:, 2 + b, 0:P]).then_inc(f_ts, 1)

            def gelu(s, b):
                act.wait_ge(f_ht, s + 1)
                nc.scalar.activation(gT[:, b, :, :].rearrange("p c t -> p (c t)"), ps[:, 4 + b, :], ACT.Gelu).then_inc(f_g, 1)

            keep_sT(0, 0)
            keep_sT(1, 1)
            with act.Fori(1, SLOTS - 2, 2) as s:
                for d in range(2):
                    gelu(s + d - 1, d)
                    keep_sT(s + d + 1, d)
            gelu(SLOTS - 3, 0)
            keep_sT(SLOTS - 1, 0)
            gelu(SLOTS - 2, 1)
            gelu(SLOTS - 1, 0)

        @block.tensor
        def _(pe):
            mm = nc.tensor.matmul
            pe.wait_ge(c_pool, 10)
            pe.wait_ge(l_attn, 32)
            for j in range(2):
                for i in range(2):
                    last = mm(ps[:, 2 * j + i, :], wqkv_sb[:, j, :], proj_bd[:, 4 * i:4 * i + 4, :].rearrange("p h f -> p (h f)"),
                              start=True, stop=True)
            last.then_inc(p_set, 1)
            nc.tensor.transpose(ps[:, 4, 0:P], wqkv_sb[:, 2, :], ident[:, :]).then_inc(p_set, 1)
            pe.wait_ge(set_dve, 1)
            pe.wait_ge(l_mod, 32)
            for j in range(2):
                last = mm(ps[:, 5, 8 * j:8 * j + B], wmod_sb[:, j * D:(j + 1) * D], siluT[:, :], start=True, stop=True)
            last.then_inc(p_set, 1)
            def turn_xn(g, first):
                pe.wait_ge(s_xn, g + 1)
                if not first:
                    pe.wait_ge(s_vbd, g)
                    pe.wait_ge(s_x2, g - 1) if not (isinstance(g, int) and g < 2) else None
                for t in range(TG):
                    last = nc.tensor.transpose(m_ps[:, t * P:(t + 1) * P], xn[:, t, :], ident[:, :])
                last.then_inc(s_xt, 1)

            turn_xn(0, True)
            pe.wait_ge(set_dve, 3)
            pe.wait_ge(set_act, 3)
            for b in range(B):
                last = mm(ps[:, b, :], silu_bc[:, b, :], wmod_sb[:, 2 * D:6 * D], start=True, stop=True)
            last.then_inc(p_set, 1)
            pe.wait_ge(set_dve, 4)
            pe.wait_ge(l_gate, 64)
            nc.tensor.transpose(ps[:, 6, 0:P], wo_perm[:, :], ident[:, :])
            nc.tensor.transpose(ps[0:GD, 6, P:2 * P], wred_sb[:, :], ident[:, :])
            nc.tensor.transpose(ps[0:GD, 6, 2 * P:2 * P + E], wg_u[:, :], ident[0:E, 0:E]).then_inc(p_set, 1)
            pe.wait_ge(set_dve, 6)
            mm(ps[:, 6, 0:E], wredT[:, :], wgT[:, :], start=True, stop=True).then_inc(p_set, 1)
            pe.wait_ge(set_dve, 7)

            def feats(g, h):
                if not (isinstance(g, int) and g == 0 and h < 2):
                    pe.wait_ge(s_phi, H * g + h - 1)
                if h == 0:
                    pe.wait_ge(s_ht, g + 1)
                for j in range(2):
                    last = mm(x_ps[h % 2][:, j, :], mix[:, j, h, :], hT[:, :], start=True, stop=True)
                last.then_inc(s_x, 1)

            def scores(g, h):
                pe.wait_ge(s_phi, H * g + h + 1)
                if not (isinstance(g, int) and g == 0 and h < 2):
                    pe.wait_ge(s_asb, H * g + h - 1)
                for t in range(TG):
                    for c_ in range(NC):
                        at = t * P + c_ * BLK
                        last = mm(a_ps[h % 2][c_ * BLK:(c_ + 1) * BLK, t * BLK:(t + 1) * BLK],
                                  phi[:, h % 4, 1, at:at + BLK], phi[:, h % 4, 0, at:at + BLK], start=True, stop=True)
                last.then_inc(s_a, 1)

            def apply_values(g, half, first):
                pe.wait_ge(s_asb, H * g + HH * (half + 1))
                pe.wait_ge(s_vbd, g + 1)
                if not first:
                    pe.wait_ge(s_on, 2 * g + half)
                for t in range(TG):
                    for q in range(HH):
                        last = mm(o_ps[q * BLK:(q + 1) * BLK, t * NC * VW:(t + 1) * NC * VW], a_sb[:, half, q, t, :],
                                  vbd[:, t, half * HH + q, :, :].rearrange("p c d -> p (c d)"), start=True, stop=True)
                last.then_inc(s_av, 1)

            def project_out(g):
                pe.wait_ge(s_ot, g + 1)
                pe.wait_ge(set_pool, 2)
                for t in range(TG):
                    last = mm(m_ps[:, t * P:(t + 1) * P], oT[:, t, :], wo_g[:, bass.ds(g, 1), :].rearrange("p a d -> p (a d)"),
                              start=True, stop=True)
                last.then_inc(s_y, 1)

            def values(g):
                pe.wait_ge(s_ht, g + 1)
                for t in range(TG):
                    last = mm(m_ps[:, t * P:(t + 1) * P], hT[:, t * P:(t + 1) * P], wvT[:, :], start=True, stop=True)
                last.then_inc(s_v, 1)

            def turn_h2(g):
                pe.wait_ge(s_h2, g + 1)
                for t in range(TG):
                    last = nc.tensor.transpose(m_ps[:, t * P:(t + 1) * P], h2m[:, t, :], ident[:, :])
                last.then_inc(s_h2t, 1)

            def gate(g):
                pe.wait_ge(s_h2ts, g + 1)
                for t in range(TG):
                    last = mm(m_ps[:, t * E:(t + 1) * E], h2T[:, t, :], w_gate[:, :], start=True, stop=True)
                last.then_inc(s_lg, 1)

            def rank(g):
                pe.wait_ge(s_pick, g + 1)
                picks = pick[:, :, :].rearrange("p t e -> p (t e)")
                mm(m_ps[:, 0:TG * E], before[:, :], picks, start=True, stop=True)
                mm(m_ps[:, TG * E:2 * TG * E], ones_b[:, :], picks, start=True, stop=True).then_inc(s_rk, 1)

            def step(g, now, prev, prev2, nxt):
                for h in range(H):
                    if h == 0 and prev2:
                        if now:
                            pe.wait_ge(s_ht, g + 1)
                        else:
                            pe.wait_ge(s_pos, g - 2)
                        turn_h2(g - 2)
                    if now:
                        feats(g, h)
                    if h < 2 and prev:
                        scores(g - 1, h + 6)
                    if h >= 2 and now:
                        scores(g, h - 2)
                    if h == 2 and prev:
                        apply_values(g - 1, 1, False)
                    if h == 2 and prev2:
                        gate(g - 2)
                    if h == 3 and now:
                        if prev2:
                            pe.wait_ge(s_lgd, g - 1)
                        values(g)
                    if h == 4 and prev:
                        if now:
                            pe.wait_ge(s_vbd, g + 1)
                        elif prev2:
                            pe.wait_ge(s_lgd, g - 1)
                        project_out(g - 1)
                    if h == 6 and prev2:
                        if prev:
                            pe.wait_ge(s_x2, g)
                        rank(g - 2)
                    if h == 6 and now:
                        apply_values(g, 0, isinstance(g, int) and g == 0)
                if nxt:
                    if prev2:
                        pe.wait_ge(s_pos, g - 1)
                    elif prev:
                        pe.wait_ge(s_x2, g)
                    turn_xn(g + 1, False)

            step(0, True, False, False, True)
            step(1, True, True, False, True)
            with pe.Fori(2, NG - 1) as g:
                step(g, True, True, True, True)
            step(NG - 1, True, True, True, False)
            step(NG, False, True, True, False)
            step(NG + 1, False, False, True, False)

            def turn_in(s, b, k):
                pe.wait_ge(f_in[b], 16 * (k + 1))
                nc.tensor.transpose(ps[:, 2 + b, 0:P], rin[:, b, 0:D], ident[:, :]).then_inc(f_t, 1)

            def expert_of(s):
                return pe.value_load(exp_i[0:1, bass.ds(s, 1)], min_val=0, max_val=E - 1)

            def hidden(s, b):
                e = expert_of(s)
                pe.wait_ge(f_ts, s + 1)
                mm(ps[:, b, :], sT[:, b, :], w1_sb[:, bass.ds(e * F, F)], start=True, stop=True).then_inc(f_h, 1)

            def turn_hidden(s, b):
                pe.wait_ge(f_hb, s + 1)
                for c_ in range(FC):
                    last = nc.tensor.transpose(ps[:, 4 + b, c_ * P:(c_ + 1) * P], hb[:, b, c_ * P:(c_ + 1) * P], ident[:, :])
                last.then_inc(f_ht, 1)

            def outer(s, b):
                e = expert_of(s)
                pe.wait_ge(f_g, s + 1)
                if not (isinstance(s, int) and s < 2):
                    pe.wait_ge(f_done, s - 1)
                for c_ in range(FC):
                    last = mm(ps[:, 6 + b, 0:D], gT[:, b, c_, :], w2_sb[:, bass.ds(e * (FC * D) + c_ * D, D)],
                              start=(c_ == 0), stop=(c_ == FC - 1))
                last.then_inc(f_y, 1)

            pe.wait_ge(s_table, 2)
            pe.wait_ge(l_exp, 64)
            pe.wait_ge(s_pos, NG)
            turn_in(0, 0, 0)
            hidden(0, 0)
            turn_in(1, 1, 0)
            def pipe(s, b, k, last=False):
                turn_hidden(s - 1, 1 - b)
                hidden(s, b)
                outer(s - 1, 1 - b)
                if not last:
                    turn_in(s + 1, 1 - b, k)

            pipe(1, 1, 1)
            pipe(2, 0, 1)
            with pe.Fori(3, SLOTS - 2, 2) as s:
                k = s // 2
                pipe(s, 1, k + 1)
                pipe(s + 1, 0, k + 1)
            pipe(SLOTS - 2, 1, (SLOTS - 1) // 2)
            pipe(SLOTS - 1, 0, 0, last=True)
            turn_hidden(SLOTS - 1, 0)
            outer(SLOTS - 1, 0)

        @block.vector
        def _(dve):
            v = nc.vector
            v.memset(pad_rec[:, 0:3 * D], 0.0)
            v.memset(pad_rec[:, 3 * D:R], float(T)).then_inc(c_dve, 1)
            dve.wait_ge(set_act, 1)
            v.tensor_scalar(ecT[:, :], ecT[:, :], 1.0, None, ALU.add).then_inc(c_dve, 1)
            dve.wait_ge(c_dve, 2)
            v.reciprocal(ecT[:, :], ecT[:, :]).then_inc(c_dve, 1)
            dve.wait_ge(c_dve, 3)
            v.tensor_tensor(siluT[:, :], cT[:, :], ecT[:, :], ALU.mult).then_inc(c_dve, 1)
            dve.wait_ge(c_dve, 4)
            v.tensor_copy(silu_bc[:, :, :], siluT[:, :].unsqueeze(2).broadcast_to([P, B, P])).then_inc(set_dve, 1)

            def norm1(g, first):
                if first:
                    dve.wait_ge(l_x0, 16)
                else:
                    dve.wait_ge(l_x, 16)
                for t in range(TG):
                    last = v.bn_stats(ln1_st[:, t, :], x_all[:, bass.ds(g * TG + t, 1), :].rearrange("p a d -> p (a d)"))
                last.then_inc(s_ln1, 1)
                dve.wait_ge(s_ln1, 3 * g + 1)
                dve.sem_inc(seq_dve, 1)
                for t in range(TG):
                    last = v.bn_aggr(ln1_mv[:, t, :], ln1_st[:, t, :])
                last.then_inc(s_ln1, 1)
                dve.wait_ge(s_ln1, 3 * g + 2)
                v.tensor_scalar(ln1_ve[:, :], ln1_mv[:, :, 1], EPS, None, ALU.add).then_inc(s_ln1, 1)

            def norm1_apply(g, first):
                dve.wait_ge(s_rs1, g + 1)
                if not first:
                    dve.wait_ge(s_xt, g)
                for t in range(TG):
                    last = v.tensor_scalar(xn[:, t, :], x_all[:, bass.ds(g * TG + t, 1), :].rearrange("p a d -> p (a d)"),
                                           ln1_mv[:, t, 0:1], ln1_rs[:, t:t + 1], ALU.subtract, ALU.mult)
                last.then_inc(s_xn, 1)

            norm1(0, True)
            norm1_apply(0, True)
            dve.wait_ge(p_set, 3)
            v.tensor_copy(modT[:, 0, :].rearrange("p (b r) -> p b r", b=B), ps[:, 5, 0:B].unsqueeze(2).broadcast_to([P, B, GB_]))
            v.tensor_scalar(modT[:, 1, :].rearrange("p (b r) -> p b r", b=B), ps[:, 5, 8:8 + B].unsqueeze(2).broadcast_to([P, B, GB_]),
                            1.0, None, ALU.add).then_inc(set_dve, 1)
            for j in range(2):
                v.tensor_copy(mix[:, 0, 4 * j:4 * j + 4, :].rearrange("p h f -> p (h f)"), ps[:, j, :])
            v.tensor_copy(wvT[:, :], ps[:, 4, 0:P]).then_inc(set_dve, 1)
            dve.wait_ge(l_gate, 64)
            v.tensor_copy(wo_perm[:, :].rearrange("p (q s d) -> p s q d", q=HH, s=2),
                          wo_sb[:, :].rearrange("p (s q d) -> p s q d", q=HH, s=2))
            v.tensor_tensor(wg_sq[:, :], wg_sb[:, :], wg_sb[:, :], ALU.mult).then_inc(c_dve, 1)
            dve.wait_ge(c_dve, 5)
            v.tensor_reduce(wg_n[:, 0:1], wg_sq[:, :], AX.X, ALU.add).then_inc(c_dve, 1)
            dve.wait_ge(c_dve, 6)
            v.tensor_scalar(wg_n[:, 1:2], wg_n[:, 0:1], 1e-8, None, ALU.max).then_inc(c_dve, 1)
            dve.wait_ge(set_pool, 1)
            v.tensor_scalar(wg_u[:, :], wg_sb[:, :], wg_n[:, 2:3], None, ALU.mult).then_inc(set_dve, 1)
            dve.wait_ge(p_set, 4)
            for b in range(B):
                last = v.tensor_copy(mod_bc[:, GB_ * b:GB_ * (b + 1), :, :].rearrange("p r j d -> p r (j d)"),
                                     ps[:, b, :].unsqueeze(1).broadcast_to([P, GB_, 4 * D]))
            last.then_inc(set_dve, 1)
            dve.wait_ge(set_dve, 5)
            v.tensor_scalar(mod_bc[:, :, 2, :], mod_bc[:, :, 2, :], 1.0, None, ALU.add)
            rows = mod_bc[:, :, 0:4:3, :]
            tmp = phi[:, :, :, :].rearrange("p a b n -> p (a b n)").rearrange("p (i g j d) -> p i g j d", i=2, g=NG, j=2)
            ab, sg = tmp[:, 0], tmp[:, 1]
            v.tensor_scalar(sg, rows, 0.0, 2.0, ALU.is_ge, ALU.mult)
            for j in range(2):
                last = v.scalar_tensor_tensor(out=ab[:, :, j, :], in0=rows[:, :, j, :], scalar=-1.0, in1=rows[:, :, j, :],
                                              op0=ALU.mult, op1=ALU.max)
            last.then_inc(c_dve, 1)
            dve.wait_ge(c_dve, 8)
            v.tensor_scalar(ab, ab, 0.25, None, ALU.max).then_inc(c_dve, 1)
            dve.wait_ge(c_dve, 9)
            for j in range(2):
                v.scalar_tensor_tensor(out=rows[:, :, j, :], in0=sg[:, :, j, :], scalar=-1.0, in1=ab[:, :, j, :],
                                       op0=ALU.add, op1=ALU.mult)
            dve.wait_ge(p_set, 5)
            v.tensor_copy(woT[:, :], ps[:, 6, 0:P])
            v.tensor_copy(wredT[:, :], ps[0:GD, 6, P:2 * P])
            v.tensor_copy(wgT[:, :], ps[0:GD, 6, 2 * P:2 * P + E]).then_inc(set_dve, 1)
            dve.wait_ge(p_set, 6)
            v.tensor_copy(w_gate[:, :], ps[:, 6, 0:E]).then_inc(set_dve, 1)
            dve.wait_ge(c_pool, 10)
            v.tensor_copy(carry[:, :], region0[:, :])
            v.tensor_copy(vbd[:, :, :, :, HD:VW].rearrange("p t h c o -> p (t h) (c o)"),
                          blk_mask[:, :, 0].unsqueeze(1).broadcast_to([P, TG * H, NC])).then_inc(c_dve, 1)

            def features(g, h):
                dve.wait_ge(s_exp, H * g + h + 1)
                if not (isinstance(g, int) and g == 0 and h < 4):
                    dve.wait_ge(s_a, H * g + h - 3)
                for j in range(2):
                    last = v.scalar_tensor_tensor(out=phi[:, h % 4, j, :], in0=x_ps[h % 2][:, j, :], scalar=0.0,
                                                  in1=ebuf[:, h % 2, j, :], op0=ALU.max, op1=ALU.add)
                last.then_inc(s_phi, 1)

            def keep_values(g, first):
                dve.wait_ge(s_v, g + 1)
                if not first:
                    dve.wait_ge(s_av, 2 * g)
                v.tensor_tensor(vbd[:, :, :, :, 0:HD].rearrange("p t h c d -> p (t h) c d"),
                                m_ps.rearrange("p (th d) -> p th d", d=HD).unsqueeze(2).broadcast_to([P, TG * H, NC, HD]),
                                blk_mask[:, :, 0:HD].unsqueeze(1).broadcast_to([P, TG * H, NC, HD]),
                                ALU.mult).then_inc(s_vbd, 1)

            def normalise(g, half):
                dve.wait_ge(s_av, 2 * g + half + 1)
                o3 = o_ps.rearrange("p (u w) -> p u w", w=VW)
                v.tensor_scalar(den[:, :], o3[:, :, HD], 1e-8, None, ALU.add).then_inc(s_nrm, 1)
                dve.wait_ge(s_nrm, 2 * (2 * g + half) + 1)
                v.reciprocal(rden[:, :], den[:, :]).then_inc(s_nrm, 1)
                dve.wait_ge(s_nrm, 2 * (2 * g + half) + 2)
                v.tensor_tensor(o_sb[:, :, half, :], o3[:, :, 0:HD], rden[:, :].unsqueeze(2).broadcast_to([P, TG * NC, HD]),
                                ALU.mult).then_inc(s_on, 1)

            def turn_o(g, first):
                dve.wait_ge(s_on, 2 * g + 2)
                if not first:
                    dve.wait_ge(s_y, g)
                v.transpose(oT[:, :, :].rearrange("p t s -> p (t s)"), o_sb[:, :, :, :].rearrange("p u s d -> p (u s d)")).then_inc(s_ot, 1)

            def residual(g):
                dve.wait_ge(s_y, g + 1)
                dve.wait_ge(s_xb, g + 1)
                v.tensor_tensor(x2[:, :, :].rearrange("p t d -> p (t d)"), m_ps, x2[:, :, :].rearrange("p t d -> p (t d)"),
                                ALU.add).then_inc(s_x2, 1)

            def norm2(g):
                dve.wait_ge(s_x2, g + 1)
                for t in range(TG):
                    last = v.bn_stats(ln2_st[:, t, :], x2[:, t, :])
                last.then_inc(s_ln2, 1)
                dve.wait_ge(s_ln2, 3 * g + 1)
                dve.sem_inc(seq_dve, 1)
                for t in range(TG):
                    last = v.bn_aggr(ln2_mv[:, t, :], ln2_st[:, t, :])
                last.then_inc(s_ln2, 1)
                dve.wait_ge(s_ln2, 3 * g + 2)
                v.tensor_scalar(ln2_ve[:, :], ln2_mv[:, :, 1], EPS, None, ALU.add).then_inc(s_ln2, 1)

            def norm2_apply(g, first):
                dve.wait_ge(s_rs2, g + 1)
                for t in range(TG):
                    last = v.tensor_scalar(h2[:, t, :], x2[:, t, :], ln2_mv[:, t, 0:1], ln2_rs[:, t:t + 1],
                                           ALU.subtract, ALU.mult)
                last.then_inc(s_nh, 1)
                dve.wait_ge(s_nh, 2 * g + 1)
                v.tensor_tensor(h2[:, :, :], h2[:, :, :], mod_bc[:, bass.ds(g, 1), 2, :].broadcast_to([P, TG, D]),
                                ALU.mult).then_inc(s_nh, 1)
                dve.wait_ge(s_nh, 2 * g + 2)
                if not first:
                    dve.wait_ge(s_h2t, g)
                    dve.wait_ge(s_rec, g)
                v.tensor_tensor(h2m[:, :, :], h2[:, :, :], mod_bc[:, bass.ds(g, 1), 1, :].broadcast_to([P, TG, D]),
                                ALU.add).then_inc(s_h2, 1)

            def route(g):
                dve.wait_ge(s_lg, g + 1)
                lg = m_ps[:, 0:TG * E].rearrange("p (t e) -> p t e", e=E)
                v.tensor_reduce(top[:, :], lg, AX.X, ALU.max).then_inc(s_rt, 1)
                dve.wait_ge(s_rt, 3 * g + 1)
                v.tensor_tensor(lgd[:, :, :], lg, top[:, :].unsqueeze(2).broadcast_to([P, TG, E]), ALU.subtract).then_inc(s_lgd, 1)
                dve.wait_ge(s_lgd, g + 1)
                v.scalar_tensor_tensor(out=cand[:, :, :], in0=lgd[:, :, :], scalar=0.0,
                                       in1=rev[:, :].unsqueeze(1).broadcast_to([P, TG, E]), op0=ALU.is_ge, op1=ALU.mult).then_inc(s_rt, 1)
                dve.wait_ge(s_rt, 3 * g + 2)
                v.tensor_reduce(cmax[:, :], cand[:, :, :], AX.X, ALU.max).then_inc(s_rt, 1)
                dve.wait_ge(s_rt, 3 * g + 3)
                v.tensor_tensor(pick[:, :, :], cand[:, :, :], cmax[:, :].unsqueeze(2).broadcast_to([P, TG, E]),
                                ALU.is_equal).then_inc(s_pick, 1)

            def gate_score(g, first):
                dve.wait_ge(s_ex, g + 1)
                v.tensor_reduce(lgs[:, :], lge[:, :, :], AX.X, ALU.add).then_inc(s_gs, 1)
                dve.wait_ge(s_gs, g + 1)
                if not first:
                    dve.wait_ge(s_gbs, g)
                v.reciprocal(score[:, :], lgs[:, :]).then_inc(s_sc, 1)

            def position(g, first):
                dve.wait_ge(s_rk, g + 1)
                rk = m_ps[:, 0:TG * E].rearrange("p (t e) -> p t e", e=E)
                ct = m_ps[:, TG * E:2 * TG * E].rearrange("p (t e) -> p t e", e=E)
                n = 7 * g
                v.tensor_copy(pref[:, 0, :], carry[:, :]).then_inc(s_ps, 1)
                for t in range(1, TG):
                    dve.wait_ge(s_ps, n + t)
                    v.tensor_tensor(pref[:, t, :], ct[:, t - 1, :], pref[:, t - 1, :], ALU.add).then_inc(s_ps, 1)
                dve.wait_ge(s_ps, n + TG)
                v.tensor_tensor(carry[:, :], ct[:, TG - 1, :], pref[:, TG - 1, :], ALU.add).then_inc(s_ps, 1)
                v.tensor_tensor(posf[:, :, :], rk, pref[:, :, :], ALU.add).then_inc(s_ps, 1)
                dve.wait_ge(s_ps, n + TG + 2)
                v.tensor_tensor(posf[:, :, :], posf[:, :, :], pick[:, :, :], ALU.mult).then_inc(s_ps, 1)
                dve.wait_ge(s_ps, n + TG + 3)
                v.tensor_reduce(posr[:, :], posf[:, :, :], AX.X, ALU.add).then_inc(s_pr, 1)
                dve.wait_ge(s_pr, g + 1)
                if not first:
                    dve.wait_ge(s_scat, 16 * TG * g)
                v.tensor_copy(pos[:, :], posr[:, :]).then_inc(s_pos, 1)

            def step(g, now, prev, prev2, nxt, first=False, firstp=False, firstp2=False):
                for h in range(H):
                    if h == 0 and nxt:
                        norm1(g + 1, False)
                    if h == 1 and nxt:
                        norm1_apply(g + 1, False)
                    if h == 3 and prev:
                        normalise(g - 1, 1)
                        turn_o(g - 1, firstp)
                    if h == 3 and prev2:
                        route(g - 2)
                    if h == 4 and now:
                        keep_values(g, first)
                    if h == 5 and prev2:
                        gate_score(g - 2, firstp2)
                    if h == 5 and prev:
                        residual(g - 1)
                        norm2(g - 1)
                    if h == 6 and prev:
                        norm2_apply(g - 1, firstp)
                    if h == 7 and prev2:
                        position(g - 2, firstp2)
                    if h == 7 and now:
                        normalise(g, 0)
                    if now:
                        features(g, h)

            step(0, True, False, False, True, first=True)
            step(1, True, True, False, True, firstp=True)
            step(2, True, True, True, True, firstp2=True)
            with dve.Fori(3, NG - 1) as g:
                step(g, True, True, True, True)
            step(NG - 1, True, True, True, False)
            step(NG, False, True, True, False)
            step(NG + 1, False, False, True, False)

            v.tensor_tensor(cnt[:, :], carry[:, :], region0[:, :], ALU.subtract)
            v.tensor_copy(carry_i[:, :], carry[:, :]).then_inc(s_table, 1)
            dve.wait_ge(s_table, 1)
            v.tensor_tensor(full[:, :, :], cnt[:, :].unsqueeze(2).broadcast_to([P, E, NT]),
                            tiles128[:, :].unsqueeze(1).broadcast_to([P, E, NT]), ALU.is_gt).then_inc(s_tab, 1)
            dve.wait_ge(s_tab, 1)
            v.tensor_reduce(nt[:, :], full[:, :, :], AX.X, ALU.add).then_inc(s_tab, 1)
            dve.wait_ge(s_tab, 2)
            v.tensor_scalar(skip[:, :], nt[:, :], -float(P), float(REGION), ALU.mult, ALU.add)
            v.tensor_copy(endt[:, 0, :], nt[:, :]).then_inc(s_tab, 1)
            src, n = 0, 3
            for sh in (1, 2, 4):
                dve.wait_ge(s_tab, n)
                v.tensor_copy(endt[:, 1 - src, 0:sh], endt[:, src, 0:sh])
                v.tensor_tensor(endt[:, 1 - src, sh:E], endt[:, src, sh:E], endt[:, src, 0:E - sh], ALU.add).then_inc(s_tab, 1)
                src, n = 1 - src, n + 1
            dve.wait_ge(s_tab, 6)
            v.tensor_tensor(past[:, :, :], slot_no[:, :].unsqueeze(2).broadcast_to([P, SLOTS, E]),
                            endt[:, src, :].unsqueeze(1).broadcast_to([P, SLOTS, E]), ALU.is_ge).then_inc(s_tab, 1)
            dve.wait_ge(s_tab, 7)
            v.tensor_tensor(hop[:, :, :], past[:, :, :], skip[:, :].unsqueeze(1).broadcast_to([P, SLOTS, E]), ALU.mult)
            v.tensor_reduce(expf[:, 0, :], past[:, :, :], AX.X, ALU.add).then_inc(s_tab, 1)
            dve.wait_ge(s_tab, 8)
            v.tensor_scalar(exp_i[:, :], expf[:, 0, :], float(E - 1), None, ALU.min)
            v.tensor_reduce(rowf[:, 0, :], hop[:, :, :], AX.X, ALU.add).then_inc(s_tab, 1)
            dve.wait_ge(s_tab, 9)
            v.scalar_tensor_tensor(out=rowf[:, 1, :], in0=slot_no[:, :], scalar=float(P), in1=rowf[:, 0, :],
                                   op0=ALU.mult, op1=ALU.add).then_inc(s_tab, 1)
            dve.wait_ge(s_tab, 10)
            v.tensor_scalar(row_i[:, :], rowf[:, 1, :], float(DUMMY), None, ALU.min).then_inc(s_table, 1)
            dve.wait_ge(s_table, 2)

            def expert_of(s):
                return dve.value_load(exp_i[0:1, bass.ds(s, 1)], min_val=0, max_val=E - 1)

            def hidden_bias(s, b):
                e = expert_of(s)
                dve.wait_ge(f_h, s + 1)
                v.tensor_tensor(hb[:, b, :], ps[:, b, :], b1_bc[:, bass.ds(e * F, F)], ALU.add).then_inc(f_hb, 1)

            def finish(s, b, k, first):
                e = expert_of(s)
                dve.wait_ge(f_y, s + 1)
                v.tensor_tensor(y1[:, b, :], ps[:, 6 + b, 0:D], b2_bc[:, bass.ds(e * D, D)], ALU.add).then_inc(f_s, 1)
                dve.wait_ge(f_s, 2 * s + 1)
                v.tensor_tensor(y2[:, b, :], y1[:, b, :], rin[:, b, 2 * D:3 * D], ALU.mult).then_inc(f_s, 1)
                dve.wait_ge(f_s, 2 * s + 2)
                if not first:
                    dve.wait_ge(f_out[b], 16 * k)
                v.tensor_copy(tok[:, b:b + 1], rin[:, b, 3 * D:R])
                v.tensor_tensor(yo[:, b, :], y2[:, b, :], rin[:, b, D:2 * D], ALU.add).then_inc(f_yd, 1)
                dve.wait_ge(f_yd, s + 1)
                dve.sem_inc(f_done, 1)

            dve.wait_ge(l_exp, 64)
            hidden_bias(0, 0)
            hidden_bias(1, 1)
            finish(0, 0, 0, True)
            hidden_bias(2, 0)
            finish(1, 1, 0, True)
            with dve.Fori(3, SLOTS - 1, 2) as s:
                k = s // 2
                hidden_bias(s, 1)
                finish(s - 1, 0, k, False)
                hidden_bias(s + 1, 0)
                finish(s, 1, k, False)
            finish(SLOTS - 1, 0, (SLOTS - 1) // 2, False)


_INS = ["L0_attn_x", "L0_attn_w_qkv", "L0_attn_w_out", "L0_attn_b_out", "L0_attn_proj", "L0_ffn_w_red", "L0_ffn_wg",
        "L0_ffn_w1", "L0_ffn_b1", "L0_ffn_w2", "L0_ffn_b2", "L0_c", "L0_wmod"]


def kernel(**inputs):
    import numpy as np
    import concourse.bacc as bacc
    from concourse.bass_utils import run_bass_kernel_spmd

    nc = bacc.Bacc("TRN2", target_bir_lowering=False, num_devices=1)
    arrays, args = {}, []
    for name in _INS:
        a = np.ascontiguousarray(inputs[name])
        if name == "L0_c":
            a = np.ascontiguousarray(a.T)
        arrays[f"in_{name}"] = a
        args.append(nc.dram_tensor(f"in_{name}", a.shape, mybir.dt.from_np(a.dtype), kind="ExternalInput").ap())
    shape = inputs["L0_attn_x"].shape
    out = nc.dram_tensor("out_0", shape, F32, kind="ExternalOutput").ap()
    adaln_kernel(nc, *args, out)
    r = run_bass_kernel_spmd(nc, [arrays], core_ids=[0])
    return r.results[0]["out_0"]
```

```python
from contextlib import ExitStack

import concourse.bass as bass
from concourse import mybir

P = 128
ALU = mybir.AluOpType
ACT = mybir.ActivationFunctionType
AX = mybir.AxisListType
F32 = mybir.dt.float32
BF16 = mybir.dt.bfloat16
I32 = mybir.dt.int32

EPS = 1e-5


def adaln_kernel(nc, x, w_qkv, w_out, b_out, proj, w_red, wg, w1, b1_t, w2, b2, c_cols, wmod, out):
    B, N, D = x.shape
    H, HD, FEAT = proj.shape
    E, _, F = w1.shape
    GD = w_red.shape[1]
    T = B * N
    NT = T // P
    TG = 4
    GT = TG * P
    NG = T // GT
    GB_ = N // GT
    BLK = 32
    NC = P // BLK
    VW = HD + 1
    HH = H // 2
    FC = F // P
    REGION = T + P
    DUMMY = E * REGION
    SLOTS = NT + E - 1
    RING = 6
    WHOLE = SLOTS // RING * RING
    HEAD = RING - 1
    BODY = HEAD + (SLOTS - 1 - HEAD) // RING * RING
    R = 3 * D + 1
    assert D == P and FEAT == P and H * HD == P and HH == NC and 2 * HD == BLK

    xf = x.rearrange("b n d -> (b n) d")
    of = out.rearrange("b n d -> (b n) d")
    sorted_rows = nc.dram_tensor("sorted_rows", [DUMMY + P, R], F32, kind="Internal").ap()

    ctx = ExitStack()
    with ctx:
        def sb(name, shape, dt=F32):
            return ctx.enter_context(nc.sbuf_tensor(name, shape, dt))

        def sem(name):
            return ctx.enter_context(nc.semaphore(name))

        x_all = sb("x_all", [P, NT, D])
        wqkv_sb = sb("wqkv_sb", [P, 3, D])
        proj_bd = sb("proj_bd", [P, H, FEAT])
        mix = sb("mix", [P, 2, H, FEAT])
        wvT = sb("wvT", [P, P])
        wo_sb = sb("wo_sb", [P, P])
        wo_perm = sb("wo_perm", [P, P])
        woT = sb("woT", [P, P])
        wo_g = sb("wo_g", [P, NG, P])
        bout_bc = sb("bout_bc", [P, D])
        wmod_sb = sb("wmod_sb", [P, 6 * D])
        cT = sb("cT", [P, B])
        ecT = sb("ecT", [P, B])
        siluT = sb("siluT", [P, B])
        silu_bc = sb("silu_bc", [P, B, P])
        modT = sb("modT", [P, 2, NG])
        mod_bc = sb("mod_bc", [P, NG, 4, D])
        wred_sb = sb("wred_sb", [P, GD])
        wredT = sb("wredT", [GD, P])
        wg_sb = sb("wg_sb", [E, GD])
        wg_sq = sb("wg_sq", [E, GD])
        wg_n = sb("wg_n", [E, 4])
        wg_u = sb("wg_u", [E, GD])
        wgT = sb("wgT", [GD, E])
        w_gate = sb("w_gate", [P, E])
        w1_sb = sb("w1_sb", [P, E * F])
        w2_sb = sb("w2_sb", [P, E * FC * D])
        b1_cols = sb("b1_cols", [P, E * FC])
        b2_bc = sb("b2_bc", [P, E * D])
        ident = sb("ident", [P, P])
        before = sb("before", [P, P], BF16)
        ones_b = sb("ones_b", [P, P], BF16)
        blk_mask = sb("blk_mask", [P, NC, VW])
        rev = sb("rev", [P, E])
        ids = sb("ids", [P, NT])
        pad_rec = sb("pad_rec", [P, R])

        ln1_st = sb("ln1_st", [P, TG, 6])
        ln1_mv = sb("ln1_mv", [P, TG, 2])
        ln1_ve = sb("ln1_ve", [P, TG])
        ln2_ve = sb("ln2_ve", [P, TG])
        neg_half = sb("neg_half", [P, TG])
        ln1_rs = sb("ln1_rs", [P, TG])
        xn = sb("xn", [P, TG, D])
        hT = sb("hT", [P, GT])
        ebuf = sb("ebuf", [P, 2, 2, GT])
        phi = sb("phi", [P, 4, 2, GT])
        a_sb = sb("a_sb", [P, 2, HH, TG, BLK])
        vbd = sb("vbd", [P, TG, H, NC, VW])
        den = sb("den", [P, TG * NC])
        rden = sb("rden", [P, TG * NC])
        o_sb = sb("o_sb", [P, TG * NC, 2, HD])
        oT = sb("oT", [P, TG, P])
        x2 = sb("x2", [P, TG, D])
        ln2_st = sb("ln2_st", [P, TG, 6])
        ln2_mv = sb("ln2_mv", [P, TG, 2])
        ln2_rs = sb("ln2_rs", [P, TG])
        h2 = sb("h2", [P, TG, D])
        h2m = sb("h2m", [P, TG, D])
        h2T = sb("h2T", [P, TG, P])
        top = sb("top", [P, TG])
        lgd = sb("lgd", [P, TG, E])
        lge = sb("lge", [P, TG, E])
        lgs = sb("lgs", [P, TG])
        score = sb("score", [P, TG])
        cand = sb("cand", [P, TG, E])
        cmax = sb("cmax", [P, TG])
        pick = sb("pick", [P, TG, E], BF16)
        carry = sb("carry", [P, E])
        pref = sb("pref", [P, TG, E])
        posf = sb("posf", [P, TG, E])
        posr = sb("posr", [P, TG])
        pos = sb("pos", [P, TG], I32)
        rec = sb("rec", [P, TG, R])

        cnt = sb("cnt", [P, E])
        full = sb("full", [P, E, NT])
        nt = sb("nt", [P, E])
        endt = sb("endt", [P, 2, E])
        skip = sb("skip", [P, E])
        past = sb("past", [P, SLOTS, E])
        hop = sb("hop", [P, SLOTS, E])
        expf = sb("expf", [P, 2, SLOTS])
        rowf = sb("rowf", [P, 2, SLOTS])
        region0 = sb("region0", [P, E])
        tiles128 = sb("tiles128", [P, NT])
        slot_no = sb("slot_no", [P, SLOTS])
        exp_i = sb("exp_i", [P, SLOTS], I32)
        row_i = sb("row_i", [P, SLOTS], I32)
        carry_i = sb("carry_i", [P, E], I32)

        rin = sb("rin", [P, RING, R])
        sT = sb("sT", [P, 2, P])
        w1_e = sb("w1_e", [P, 2, F])
        gT = sb("gT", [P, 2, FC, P])
        y1 = sb("y1", [P, 2, D])
        y2 = sb("y2", [P, 2, D])
        yo = sb("yo", [P, RING, D])
        tok = sb("tok", [P, RING], I32)

        ps = ctx.enter_context(nc.psum_tensor("ps", [P, 8, 512], F32))
        x_ps = [ps[:, 2 * i:2 * i + 2, :] for i in range(2)]
        a_ps = [ps[:, 4 + i, 0:GT // NC] for i in range(2)]
        o_ps = ps[:, 6, 0:TG * NC * VW]
        h_ps = [ps[:, 4 * i:4 * i + 2, :] for i in range(2)]
        m_ps = ps[:, 7, :]

        l_attn = sem("l_attn"); l_mod = sem("l_mod"); l_gate = sem("l_gate"); l_x0 = sem("l_x0"); l_x = sem("l_x")
        l_exp = sem("l_exp"); l_pad = sem("l_pad")
        c_pool = sem("c_pool"); c_dve = sem("c_dve"); p_set = sem("p_set"); set_dve = sem("set_dve"); set_act = sem("set_act")
        set_pool = sem("set_pool")
        s_x = sem("s_x"); s_a = sem("s_a"); s_av = sem("s_av"); s_y = sem("s_y"); s_xt = sem("s_xt")
        s_v = sem("s_v"); s_h2t = sem("s_h2t"); s_lg = sem("s_lg"); s_rk = sem("s_rk")
        s_exp = sem("s_exp"); s_asb = sem("s_asb"); s_ht = sem("s_ht"); s_h2ts = sem("s_h2ts"); s_ex = sem("s_ex")
        s_neg = sem("s_neg"); s_xb = sem("s_xb"); s_rec = sem("s_rec"); s_gbs = sem("s_gbs"); s_scat = sem("s_scat")
        s_phi = sem("s_phi"); s_ln1 = sem("s_ln1"); s_xn = sem("s_xn"); s_vbd = sem("s_vbd"); s_nrm = sem("s_nrm")
        s_on = sem("s_on"); s_ot = sem("s_ot"); s_x2 = sem("s_x2"); s_ln2 = sem("s_ln2"); s_h2 = sem("s_h2")
        s_rt = sem("s_rt"); s_pick = sem("s_pick"); s_sc = sem("s_sc"); s_lgd = sem("s_lgd"); s_ps = sem("s_ps"); s_pos = sem("s_pos")
        s_nh = sem("s_nh"); s_gs = sem("s_gs"); s_pr = sem("s_pr"); f_s = sem("f_s"); seq_pool = sem("seq_pool"); seq_dve = sem("seq_dve"); s_rs1 = sem("s_rs1"); s_rs2 = sem("s_rs2"); s_tab = sem("s_tab"); s_table = sem("s_table"); s_tail = sem("s_tail")
        f_in = [sem(f"f_in{b}") for b in range(RING)]
        f_t = sem("f_t"); f_ts = sem("f_ts"); f_w = sem("f_w"); f_h = sem("f_h"); f_g = sem("f_g")
        f_y = sem("f_y"); f_yd = sem("f_yd"); f_tok = sem("f_tok"); 
        f_out = [sem(f"f_out{b}") for b in range(RING)]

        block = ctx.enter_context(nc.Block())

        @block.sync
        def _(sp):
            sp.dma_start(wqkv_sb[:, :, :], w_qkv.rearrange("(j r) d -> r j d", j=3)).then_inc(l_attn, 16)
            sp.dma_start(proj_bd[:, 0, :], proj.rearrange("h k f -> (h k) f")).then_inc(l_attn, 16)
            sp.dma_start(cT[:, :], c_cols).then_inc(l_mod, 16)
            sp.dma_start(wmod_sb[:, :], wmod).then_inc(l_mod, 16)
            xt = xf.rearrange("(t p) d -> p t d", p=P)
            sp.dma_start(x_all[:, 0:TG, :], xt[:, 0:TG, :]).then_inc(l_x0, 16)
            sp.dma_start(wo_sb[:, :], w_out).then_inc(l_gate, 16)
            sp.dma_start(bout_bc[:, :], b_out.rearrange("(a d) -> a d", a=1).partition_broadcast(P)).then_inc(l_gate, 16)
            sp.dma_start(wred_sb[:, :], w_red).then_inc(l_gate, 16)
            sp.dma_start(wg_sb[:, :], wg).then_inc(l_gate, 16)
            sp.dma_start(x_all[:, TG:NT, :], xt[:, TG:NT, :]).then_inc(l_x, 16)
            sp.dma_start(w1_sb[:, :].rearrange("p (e f) -> p e f", e=E), w1.rearrange("e d f -> d e f")).then_inc(l_exp, 16)
            sp.dma_start(w2_sb[:, :].rearrange("p (e c d) -> p e c d", e=E, c=FC),
                         w2.rearrange("e (c p) d -> p e c d", p=P)).then_inc(l_exp, 16)
            sp.dma_start(b1_cols[:, :], b1_t).then_inc(l_exp, 16)
            sp.dma_start(b2_bc[:, :], b2.rearrange("(a e) f -> a (e f)", a=1).partition_broadcast(P)).then_inc(l_exp, 16)
            sp.wait_ge(c_dve, 1)
            sp.dma_start(sorted_rows[DUMMY:DUMMY + P, :], pad_rec[:, :]).then_inc(s_tail, 16)
            sp.wait_ge(s_table, 1)
            for e in range(E):
                row = sp.value_load(carry_i[0:1, e:e + 1], min_val=e * REGION, max_val=e * REGION + T)
                sp.dma_start(sorted_rows[bass.ds(row, P), :], pad_rec[:, :]).then_inc(s_tail, 16)
            sp.wait_ge(s_tail, 16 * (E + 1))
            sp.wait_ge(s_scat, 16 * NT)
            sp.wait_ge(s_table, 2)

            def load_slot(s, b):
                row = sp.value_load(row_i[0:1, bass.ds(s, 1)], min_val=0, max_val=DUMMY)
                sp.dma_start(rin[:, b, :], sorted_rows[bass.ds(row, P), :]).then_inc(f_in[b], 16)

            def reload_slot(s, b):
                sp.wait_ge(f_yd, s - RING + 1)
                load_slot(s, b)

            for s in range(RING):
                load_slot(s, s)
            with sp.Fori(RING, WHOLE - RING + 1, RING) as s:
                for b in range(RING):
                    reload_slot(s + b, b)
            for s in range(WHOLE, SLOTS):
                reload_slot(s, s % RING)

        @block.gpsimd
        def _(pool):
            g_ = nc.gpsimd
            g_.memset(ident[:, :], 0.0).then_inc(c_pool, 1)
            g_.memset(ones_b[:, :], 1.0).then_inc(c_pool, 1)
            g_.memset(blk_mask[:, :, :], 1.0).then_inc(c_pool, 1)
            g_.memset(neg_half[:, :], -0.5)
            g_.iota(tiles128[:, :], [[P, NT]], base=0, channel_multiplier=0, allow_small_or_imprecise_dtypes=True)
            g_.iota(region0[:, :], [[REGION, E]], base=0, channel_multiplier=0, allow_small_or_imprecise_dtypes=True)
            g_.iota(slot_no[:, :], [[1, SLOTS]], base=0, channel_multiplier=0, allow_small_or_imprecise_dtypes=True)
            g_.iota(rev[:, :], [[-1, E]], base=E, channel_multiplier=0, allow_small_or_imprecise_dtypes=True)
            g_.iota(ids[:, :], [[P, NT]], base=0, channel_multiplier=1,
                    allow_small_or_imprecise_dtypes=True).then_inc(c_pool, 1)
            pool.wait_ge(c_pool, 4)
            g_.affine_select(out=ident[:, :], in_=ident[:, :], compare_op=ALU.not_equal, fill=1.0,
                             base=0, pattern=[[-1, P]], channel_multiplier=1).then_inc(c_pool, 1)
            g_.affine_select(out=before[:, :], in_=ones_b[:, :], compare_op=ALU.is_gt, fill=0.0,
                             base=0, pattern=[[1, P]], channel_multiplier=-1).then_inc(c_pool, 1)
            g_.affine_select(out=blk_mask[:, :, :], in_=blk_mask[:, :, :], compare_op=ALU.is_ge, fill=0.0,
                             base=0, pattern=[[-BLK, NC], [0, VW]], channel_multiplier=1).then_inc(c_pool, 1)
            pool.wait_ge(c_pool, 7)
            g_.affine_select(out=blk_mask[:, :, :], in_=blk_mask[:, :, :], compare_op=ALU.is_ge, fill=0.0,
                             base=BLK - 1, pattern=[[BLK, NC], [0, VW]], channel_multiplier=-1).then_inc(c_pool, 1)
            pool.wait_ge(l_attn, 32)
            g_.affine_select(out=proj_bd[:, 1:H, :], in_=proj_bd[:, 0:1, :].broadcast_to([P, H - 1, FEAT]),
                             compare_op=ALU.is_ge, fill=0.0, base=-HD,
                             pattern=[[-HD, H - 1], [0, FEAT]], channel_multiplier=1).then_inc(c_pool, 1)
            pool.wait_ge(c_pool, 9)
            g_.affine_select(out=proj_bd[:, :, :], in_=proj_bd[:, :, :], compare_op=ALU.is_ge, fill=0.0,
                             base=HD - 1, pattern=[[HD, H], [0, FEAT]], channel_multiplier=-1).then_inc(c_pool, 1)

            def rsqrt(out, in_, done):
                n = in_.shape[0]
                g_.tensor_tensor(out, in_, neg_half[0:n, 0:in_.shape[1]], ALU.pow).then_inc(done, 1)

            pool.wait_ge(s_ln1, 3)
            rsqrt(ln1_rs[:, :], ln1_ve[:, :], s_rs1)
            pool.wait_ge(c_dve, 7)
            rsqrt(wg_n[:, 2:3], wg_n[:, 1:2], set_pool)
            pool.wait_ge(set_dve, 6)
            g_.tensor_tensor(wo_g[:, :, :], woT[:, :].unsqueeze(1).broadcast_to([P, NG, P]), mod_bc[:, :, 0, :],
                             ALU.mult).then_inc(set_pool, 1)
            pool.wait_ge(set_pool, 2)
            g_.tensor_tensor(mod_bc[:, :, 0, :], mod_bc[:, :, 0, :],
                             bout_bc[:, :].unsqueeze(1).broadcast_to([P, NG, D]), ALU.mult).then_inc(set_pool, 1)

            def wait_then(s, value):
                pool.wait_ge(s, value)
                pool.sem_inc(seq_pool, 1)

            def residual_base(g):
                pool.wait_ge(l_x, 16)
                pool.wait_ge(l_x0, 16)
                pool.wait_ge(set_pool, 3)
                g_.tensor_tensor(x2[:, :, :], x_all[:, bass.ds(g * TG, TG), :],
                                 mod_bc[:, bass.ds(g, 1), 0, :].broadcast_to([P, TG, D]), ALU.add).then_inc(s_xb, 1)

            def build_records(g, first):
                pool.wait_ge(s_h2, g + 1)
                if not first:
                    wait_then(s_scat, 16 * TG * g)
                g_.tensor_copy(rec[:, :, 0:D], h2m[:, :, :])
                g_.tensor_copy(rec[:, :, D:2 * D], x2[:, :, :])
                g_.tensor_copy(rec[:, :, 3 * D:3 * D + 1], ids[:, bass.ds(g * TG, TG)].unsqueeze(2)).then_inc(s_rec, 1)

            def build_scale(g):
                pool.wait_ge(s_sc, g + 1)
                g_.tensor_tensor(rec[:, :, 2 * D:3 * D], mod_bc[:, bass.ds(g, 1), 3, :].broadcast_to([P, TG, D]),
                                 score[:, :].unsqueeze(2).broadcast_to([P, TG, D]), ALU.mult).then_inc(s_gbs, 1)

            def scatter(g):
                pool.wait_ge(s_pos, g + 1)
                pool.wait_ge(s_gbs, g + 1)
                wait_then(s_rec, g + 1)
                for t in range(TG):
                    g_.indirect_dma_start(out=sorted_rows[:, :],
                                          out_offset=bass.IndirectOffsetOnAxis(ap=pos[:, t:t + 1], axis=0),
                                          in_=rec[:, t, :], in_offset=None).then_inc(s_scat, 16)

            def step(g, now, prev, prev2, first2=False, nxt=True):
                for h in range(H):
                    if h == 0 and nxt:
                        pool.wait_ge(s_ln1, 3 * g + 6)
                        rsqrt(ln1_rs[:, :], ln1_ve[:, :], s_rs1)
                    if h == 5 and prev:
                        pool.wait_ge(s_ln2, 3 * g)
                        rsqrt(ln2_rs[:, :], ln2_ve[:, :], s_rs2)
                    if h == 1 and prev2:
                        build_records(g - 2, first2)
                    if h == 3 and prev:
                        if prev2:
                            pool.wait_ge(s_rec, g - 1)
                        residual_base(g - 1)
                    if h == 5 and prev2:
                        build_scale(g - 2)
                    if h == 7 and prev2:
                        scatter(g - 2)

            step(0, True, False, False)
            step(1, True, True, False)
            step(2, True, True, True, first2=True)
            with pool.Fori(3, NG - 1) as g:
                step(g, True, True, True)
            step(NG - 1, True, True, True, nxt=False)
            step(NG, False, True, True, nxt=False)
            step(NG + 1, False, False, True, nxt=False)

            def put(s, b):
                wait_then(f_yd, s + 1)
                g_.indirect_dma_start(out=of[:, :], out_offset=bass.IndirectOffsetOnAxis(ap=tok[:, b:b + 1], axis=0),
                                      in_=yo[:, b, :], in_offset=None, bounds_check=T - 1,
                                      oob_is_err=False).then_inc(f_out[b], 16)

            with pool.Fori(0, WHOLE - RING + 1, RING) as s:
                for b in range(RING):
                    put(s + b, b)
            for s in range(WHOLE, SLOTS):
                put(s, s % RING)
            for b in range(RING):
                pool.wait_ge(f_out[b], 16 * ((SLOTS - b + RING - 1) // RING))

        @block.scalar
        def _(act):
            act.wait_ge(l_mod, 32)
            nc.scalar.activation(ecT[:, :], cT[:, :], ACT.Exp, scale=-1.0).then_inc(set_act, 1)
            act.wait_ge(p_set, 1)
            for j in range(2):
                nc.scalar.copy(mix[:, 1, 4 * j:4 * j + 4, :].rearrange("p h f -> p (h f)"), ps[:, 2 + j, :]).then_inc(set_act, 1)

            def exp_head(g, h):
                act.wait_ge(s_x, H * g + h + 1)
                if not (isinstance(g, int) and g == 0 and h < 2):
                    act.wait_ge(s_phi, H * g + h - 1)
                nc.scalar.activation(ebuf[:, h % 2, :, :], x_ps[h % 2], ACT.Relu, scale=-1.0).then_inc(s_neg, 1)
                act.wait_ge(s_neg, H * g + h + 1)
                nc.scalar.activation(ebuf[:, h % 2, :, :], ebuf[:, h % 2, :, :], ACT.Exp, scale=-1.0).then_inc(s_exp, 1)

            def keep_a(g, h, first):
                act.wait_ge(s_a, H * g + h + 1)
                if h % HH == 0 and not first:
                    act.wait_ge(s_av, 2 * g + h // HH - 1)
                nc.scalar.copy(a_sb[:, h // HH, h % HH, :, :], a_ps[h % 2].rearrange("p (t s) -> p t s", t=TG)).then_inc(s_asb, 1)

            def keep_hT(g, first):
                act.wait_ge(s_xt, g + 1)
                if first:
                    act.wait_ge(set_dve, 2)
                else:
                    act.wait_ge(s_x, H * g)
                nc.scalar.activation(hT[:, :], m_ps, ACT.Identity, bias=modT[:, 0, bass.ds(g, 1)],
                                     scale=modT[:, 1, bass.ds(g, 1)]).then_inc(s_ht, 1)

            def keep_h2T(g):
                act.wait_ge(s_h2t, g + 1)
                nc.scalar.copy(h2T[:, :, :].rearrange("p t d -> p (t d)"), m_ps).then_inc(s_h2ts, 1)

            def gate_exp(g):
                act.wait_ge(s_lgd, g + 1)
                nc.scalar.activation(lge[:, :, :], lgd[:, :, :], ACT.Exp).then_inc(s_ex, 1)

            def step(g, now, prev, prev2, nxt, first=False, first2=False):
                for h in range(H):
                    if h == 0 and prev2:
                        keep_h2T(g - 2)
                    if now:
                        exp_head(g, h)
                    if h == 3 and prev2:
                        gate_exp(g - 2)
                    if h < 2 and prev:
                        keep_a(g - 1, h + 6, first2)
                    if h >= 2 and now:
                        keep_a(g, h - 2, first)
                if nxt:
                    keep_hT(g + 1, False)

            keep_hT(0, True)
            step(0, True, False, False, True, first=True)
            step(1, True, True, False, True, first2=True)
            with act.Fori(2, NG - 1) as g:
                step(g, True, True, True, True)
            step(NG - 1, True, True, True, False)
            step(NG, False, True, True, False)
            step(NG + 1, False, False, True, False)

            def keep_in(s, b):
                if not (isinstance(s, int) and s < 2):
                    act.wait_ge(f_h, 2 * (s - 1))
                act.wait_ge(f_t, s + 1)
                nc.scalar.copy(sT[:, b, :], ps[:, 2 + b, 0:P]).then_inc(f_ts, 1)

            def gelu(s, b):
                e = act.value_load(exp_i[0:1, bass.ds(s, 1)], min_val=0, max_val=E - 1)
                for j in range(FC // 2):
                    act.wait_ge(f_h, 2 * s + j + 1)
                    for i in range(2):
                        c_ = 2 * j + i
                        last = nc.scalar.activation(gT[:, b, c_, :], h_ps[b][:, j, i * P:(i + 1) * P], ACT.Gelu,
                                                    bias=b1_cols[:, bass.ds(e * FC + c_, 1)])
                    last.then_inc(f_g, 1)

            act.wait_ge(s_table, 2)
            act.wait_ge(l_exp, 64)
            keep_in(0, 0)
            with act.Fori(0, WHOLE - RING + 1, RING) as s:
                for b in range(RING):
                    keep_in(s + b + 1, (b + 1) % 2)
                    gelu(s + b, b % 2)
            for s in range(WHOLE, SLOTS):
                if s + 1 < SLOTS:
                    keep_in(s + 1, (s + 1) % 2)
                gelu(s, s % 2)

        @block.tensor
        def _(pe):
            mm = nc.tensor.matmul
            pe.wait_ge(c_pool, 10)
            pe.wait_ge(l_attn, 32)
            for j in range(2):
                for i in range(2):
                    last = mm(ps[:, 2 * j + i, :], wqkv_sb[:, j, :], proj_bd[:, 4 * i:4 * i + 4, :].rearrange("p h f -> p (h f)"),
                              start=True, stop=True)
            last.then_inc(p_set, 1)
            nc.tensor.transpose(ps[:, 4, 0:P], wqkv_sb[:, 2, :], ident[:, :]).then_inc(p_set, 1)
            pe.wait_ge(set_dve, 1)
            pe.wait_ge(l_mod, 32)
            for j in range(2):
                last = mm(ps[:, 5, 8 * j:8 * j + B], wmod_sb[:, j * D:(j + 1) * D], siluT[:, :], start=True, stop=True)
            last.then_inc(p_set, 1)
            def turn_xn(g, first):
                pe.wait_ge(s_xn, g + 1)
                if not first:
                    pe.wait_ge(s_vbd, g)
                    pe.wait_ge(s_x2, g - 1) if not (isinstance(g, int) and g < 2) else None
                for t in range(TG):
                    last = nc.tensor.transpose(m_ps[:, t * P:(t + 1) * P], xn[:, t, :], ident[:, :])
                last.then_inc(s_xt, 1)

            turn_xn(0, True)
            pe.wait_ge(set_dve, 3)
            pe.wait_ge(set_act, 3)
            for b in range(B):
                last = mm(ps[:, b, :], silu_bc[:, b, :], wmod_sb[:, 2 * D:6 * D], start=True, stop=True)
            last.then_inc(p_set, 1)
            pe.wait_ge(set_dve, 4)
            pe.wait_ge(l_gate, 64)
            nc.tensor.transpose(ps[:, 6, 0:P], wo_perm[:, :], ident[:, :])
            nc.tensor.transpose(ps[0:GD, 6, P:2 * P], wred_sb[:, :], ident[:, :])
            nc.tensor.transpose(ps[0:GD, 6, 2 * P:2 * P + E], wg_u[:, :], ident[0:E, 0:E]).then_inc(p_set, 1)
            pe.wait_ge(set_dve, 6)
            mm(ps[:, 6, 0:E], wredT[:, :], wgT[:, :], start=True, stop=True).then_inc(p_set, 1)
            pe.wait_ge(set_dve, 7)

            def feats(g, h):
                if not (isinstance(g, int) and g == 0 and h < 2):
                    pe.wait_ge(s_phi, H * g + h - 1)
                if h == 0:
                    pe.wait_ge(s_ht, g + 1)
                for j in range(2):
                    last = mm(x_ps[h % 2][:, j, :], mix[:, j, h, :], hT[:, :], start=True, stop=True)
                last.then_inc(s_x, 1)

            def scores(g, h):
                pe.wait_ge(s_phi, H * g + h + 1)
                if not (isinstance(g, int) and g == 0 and h < 2):
                    pe.wait_ge(s_asb, H * g + h - 1)
                for t in range(TG):
                    for c_ in range(NC):
                        at = t * P + c_ * BLK
                        last = mm(a_ps[h % 2][c_ * BLK:(c_ + 1) * BLK, t * BLK:(t + 1) * BLK],
                                  phi[:, h % 4, 1, at:at + BLK], phi[:, h % 4, 0, at:at + BLK], start=True, stop=True)
                last.then_inc(s_a, 1)

            def apply_values(g, half, first):
                pe.wait_ge(s_asb, H * g + HH * (half + 1))
                pe.wait_ge(s_vbd, g + 1)
                if not first:
                    pe.wait_ge(s_on, 2 * g + half)
                for t in range(TG):
                    for q in range(HH):
                        last = mm(o_ps[q * BLK:(q + 1) * BLK, t * NC * VW:(t + 1) * NC * VW], a_sb[:, half, q, t, :],
                                  vbd[:, t, half * HH + q, :, :].rearrange("p c d -> p (c d)"), start=True, stop=True)
                last.then_inc(s_av, 1)

            def project_out(g):
                pe.wait_ge(s_ot, g + 1)
                pe.wait_ge(set_pool, 2)
                for t in range(TG):
                    last = mm(m_ps[:, t * P:(t + 1) * P], oT[:, t, :], wo_g[:, bass.ds(g, 1), :].rearrange("p a d -> p (a d)"),
                              start=True, stop=True)
                last.then_inc(s_y, 1)

            def values(g):
                pe.wait_ge(s_ht, g + 1)
                for t in range(TG):
                    last = mm(m_ps[:, t * P:(t + 1) * P], hT[:, t * P:(t + 1) * P], wvT[:, :], start=True, stop=True)
                last.then_inc(s_v, 1)

            def turn_h2(g):
                pe.wait_ge(s_h2, g + 1)
                for t in range(TG):
                    last = nc.tensor.transpose(m_ps[:, t * P:(t + 1) * P], h2m[:, t, :], ident[:, :])
                last.then_inc(s_h2t, 1)

            def gate(g):
                pe.wait_ge(s_h2ts, g + 1)
                for t in range(TG):
                    last = mm(m_ps[:, t * E:(t + 1) * E], h2T[:, t, :], w_gate[:, :], start=True, stop=True)
                last.then_inc(s_lg, 1)

            def rank(g):
                pe.wait_ge(s_pick, g + 1)
                picks = pick[:, :, :].rearrange("p t e -> p (t e)")
                mm(m_ps[:, 0:TG * E], before[:, :], picks, start=True, stop=True)
                mm(m_ps[:, TG * E:2 * TG * E], ones_b[:, :], picks, start=True, stop=True).then_inc(s_rk, 1)

            def step(g, now, prev, prev2, nxt):
                for h in range(H):
                    if h == 0 and prev2:
                        if now:
                            pe.wait_ge(s_ht, g + 1)
                        else:
                            pe.wait_ge(s_pos, g - 2)
                        turn_h2(g - 2)
                    if now:
                        feats(g, h)
                    if h < 2 and prev:
                        scores(g - 1, h + 6)
                    if h >= 2 and now:
                        scores(g, h - 2)
                    if h == 2 and prev:
                        apply_values(g - 1, 1, False)
                    if h == 2 and prev2:
                        gate(g - 2)
                    if h == 3 and now:
                        if prev2:
                            pe.wait_ge(s_lgd, g - 1)
                        values(g)
                    if h == 4 and prev:
                        if now:
                            pe.wait_ge(s_vbd, g + 1)
                        elif prev2:
                            pe.wait_ge(s_lgd, g - 1)
                        project_out(g - 1)
                    if h == 6 and prev2:
                        if prev:
                            pe.wait_ge(s_x2, g)
                        rank(g - 2)
                    if h == 6 and now:
                        apply_values(g, 0, isinstance(g, int) and g == 0)
                if nxt:
                    if prev2:
                        pe.wait_ge(s_pos, g - 1)
                    elif prev:
                        pe.wait_ge(s_x2, g)
                    turn_xn(g + 1, False)

            step(0, True, False, False, True)
            step(1, True, True, False, True)
            with pe.Fori(2, NG - 1) as g:
                step(g, True, True, True, True)
            step(NG - 1, True, True, True, False)
            step(NG, False, True, True, False)
            step(NG + 1, False, False, True, False)

            def turn_in(s, b, k):
                pe.wait_ge(f_in[b], 16 * (k + 1))
                if not (isinstance(s, int) and s < 2):
                    pe.wait_ge(f_ts, s - 1)
                nc.tensor.transpose(ps[:, 2 + b % 2, 0:P], rin[:, b, 0:D], ident[:, :]).then_inc(f_t, 1)

            def hidden(s, b):
                if not (isinstance(s, int) and s < 2):
                    pe.wait_ge(f_g, 2 * (s - 1))
                pe.wait_ge(f_w, s + 1)
                pe.wait_ge(f_ts, s + 1)
                for j in range(FC // 2):
                    for i in range(2):
                        c_ = 2 * j + i
                        last = mm(h_ps[b % 2][:, j, i * P:(i + 1) * P], w1_e[:, b % 2, c_ * P:(c_ + 1) * P], sT[:, b % 2, :],
                                  start=True, stop=True)
                    last.then_inc(f_h, 1)

            def outer(s, b):
                e = pe.value_load(exp_i[0:1, bass.ds(s, 1)], min_val=0, max_val=E - 1)
                if not (isinstance(s, int) and s < 2):
                    pe.wait_ge(f_s, 2 * (s - 2) + 1)
                for c_ in range(FC):
                    if c_ % 2 == 0:
                        pe.wait_ge(f_g, 2 * s + c_ // 2 + 1)
                    last = mm(ps[:, 6 + b % 2, 0:D], gT[:, b % 2, c_, :], w2_sb[:, bass.ds(e * (FC * D) + c_ * D, D)],
                              start=(c_ == 0), stop=(c_ == FC - 1))
                last.then_inc(f_y, 1)

            pe.wait_ge(s_table, 2)
            pe.wait_ge(l_exp, 64)
            pe.wait_ge(s_pos, NG)
            turn_in(0, 0, 0)
            turn_in(1, 1, 0)
            hidden(0, 0)

            def pipe(s, b, k):
                turn_in(s + 1, (b + 1) % RING, k)
                hidden(s, b)
                outer(s - 1, (b - 1) % RING)

            for s in range(1, HEAD):
                pipe(s, s % RING, (s + 1) // RING)
            with pe.Fori(HEAD, BODY - RING + 1, RING) as s:
                for d in range(RING):
                    pipe(s + d, (HEAD + d) % RING, (s + d + 1) // RING)
            for s in range(BODY, SLOTS - 1):
                pipe(s, s % RING, (s + 1) // RING)
            hidden(SLOTS - 1, (SLOTS - 1) % RING)
            outer(SLOTS - 2, (SLOTS - 2) % RING)
            outer(SLOTS - 1, (SLOTS - 1) % RING)

        @block.vector
        def _(dve):
            v = nc.vector
            v.memset(pad_rec[:, 0:3 * D], 0.0)
            v.memset(pad_rec[:, 3 * D:R], float(T)).then_inc(c_dve, 1)
            dve.wait_ge(set_act, 1)
            v.tensor_scalar(ecT[:, :], ecT[:, :], 1.0, None, ALU.add).then_inc(c_dve, 1)
            dve.wait_ge(c_dve, 2)
            v.reciprocal(ecT[:, :], ecT[:, :]).then_inc(c_dve, 1)
            dve.wait_ge(c_dve, 3)
            v.tensor_tensor(siluT[:, :], cT[:, :], ecT[:, :], ALU.mult).then_inc(c_dve, 1)
            dve.wait_ge(c_dve, 4)
            v.tensor_copy(silu_bc[:, :, :], siluT[:, :].unsqueeze(2).broadcast_to([P, B, P])).then_inc(set_dve, 1)

            def norm1(g, first):
                if first:
                    dve.wait_ge(l_x0, 16)
                else:
                    dve.wait_ge(l_x, 16)
                for t in range(TG):
                    last = v.bn_stats(ln1_st[:, t, :], x_all[:, bass.ds(g * TG + t, 1), :].rearrange("p a d -> p (a d)"))
                last.then_inc(s_ln1, 1)
                dve.wait_ge(s_ln1, 3 * g + 1)
                dve.sem_inc(seq_dve, 1)
                for t in range(TG):
                    last = v.bn_aggr(ln1_mv[:, t, :], ln1_st[:, t, :])
                last.then_inc(s_ln1, 1)
                dve.wait_ge(s_ln1, 3 * g + 2)
                v.tensor_scalar(ln1_ve[:, :], ln1_mv[:, :, 1], EPS, None, ALU.add).then_inc(s_ln1, 1)

            def norm1_apply(g, first):
                dve.wait_ge(s_rs1, g + 1)
                if not first:
                    dve.wait_ge(s_xt, g)
                for t in range(TG):
                    last = v.tensor_scalar(xn[:, t, :], x_all[:, bass.ds(g * TG + t, 1), :].rearrange("p a d -> p (a d)"),
                                           ln1_mv[:, t, 0:1], ln1_rs[:, t:t + 1], ALU.subtract, ALU.mult)
                last.then_inc(s_xn, 1)

            norm1(0, True)
            norm1_apply(0, True)
            dve.wait_ge(p_set, 3)
            v.tensor_copy(modT[:, 0, :].rearrange("p (b r) -> p b r", b=B), ps[:, 5, 0:B].unsqueeze(2).broadcast_to([P, B, GB_]))
            v.tensor_scalar(modT[:, 1, :].rearrange("p (b r) -> p b r", b=B), ps[:, 5, 8:8 + B].unsqueeze(2).broadcast_to([P, B, GB_]),
                            1.0, None, ALU.add).then_inc(set_dve, 1)
            for j in range(2):
                v.tensor_copy(mix[:, 0, 4 * j:4 * j + 4, :].rearrange("p h f -> p (h f)"), ps[:, j, :])
            v.tensor_copy(wvT[:, :], ps[:, 4, 0:P]).then_inc(set_dve, 1)
            dve.wait_ge(l_gate, 64)
            v.tensor_copy(wo_perm[:, :].rearrange("p (q s d) -> p s q d", q=HH, s=2),
                          wo_sb[:, :].rearrange("p (s q d) -> p s q d", q=HH, s=2))
            v.tensor_tensor(wg_sq[:, :], wg_sb[:, :], wg_sb[:, :], ALU.mult).then_inc(c_dve, 1)
            dve.wait_ge(c_dve, 5)
            v.tensor_reduce(wg_n[:, 0:1], wg_sq[:, :], AX.X, ALU.add).then_inc(c_dve, 1)
            dve.wait_ge(c_dve, 6)
            v.tensor_scalar(wg_n[:, 1:2], wg_n[:, 0:1], 1e-8, None, ALU.max).then_inc(c_dve, 1)
            dve.wait_ge(set_pool, 1)
            v.tensor_scalar(wg_u[:, :], wg_sb[:, :], wg_n[:, 2:3], None, ALU.mult).then_inc(set_dve, 1)
            dve.wait_ge(p_set, 4)
            for b in range(B):
                last = v.tensor_copy(mod_bc[:, GB_ * b:GB_ * (b + 1), :, :].rearrange("p r j d -> p r (j d)"),
                                     ps[:, b, :].unsqueeze(1).broadcast_to([P, GB_, 4 * D]))
            last.then_inc(set_dve, 1)
            dve.wait_ge(set_dve, 5)
            v.tensor_scalar(mod_bc[:, :, 2, :], mod_bc[:, :, 2, :], 1.0, None, ALU.add)
            rows = mod_bc[:, :, 0:4:3, :]
            tmp = phi[:, :, :, :].rearrange("p a b n -> p (a b n)").rearrange("p (i g j d) -> p i g j d", i=2, g=NG, j=2)
            ab, sg = tmp[:, 0], tmp[:, 1]
            v.tensor_scalar(sg, rows, 0.0, 2.0, ALU.is_ge, ALU.mult)
            for j in range(2):
                last = v.scalar_tensor_tensor(out=ab[:, :, j, :], in0=rows[:, :, j, :], scalar=-1.0, in1=rows[:, :, j, :],
                                              op0=ALU.mult, op1=ALU.max)
            last.then_inc(c_dve, 1)
            dve.wait_ge(c_dve, 8)
            v.tensor_scalar(ab, ab, 0.25, None, ALU.max).then_inc(c_dve, 1)
            dve.wait_ge(c_dve, 9)
            for j in range(2):
                v.scalar_tensor_tensor(out=rows[:, :, j, :], in0=sg[:, :, j, :], scalar=-1.0, in1=ab[:, :, j, :],
                                       op0=ALU.add, op1=ALU.mult)
            dve.wait_ge(p_set, 5)
            v.tensor_copy(woT[:, :], ps[:, 6, 0:P])
            v.tensor_copy(wredT[:, :], ps[0:GD, 6, P:2 * P])
            v.tensor_copy(wgT[:, :], ps[0:GD, 6, 2 * P:2 * P + E]).then_inc(set_dve, 1)
            dve.wait_ge(p_set, 6)
            v.tensor_copy(w_gate[:, :], ps[:, 6, 0:E]).then_inc(set_dve, 1)
            dve.wait_ge(c_pool, 10)
            v.tensor_copy(carry[:, :], region0[:, :])
            v.tensor_copy(vbd[:, :, :, :, HD:VW].rearrange("p t h c o -> p (t h) (c o)"),
                          blk_mask[:, :, 0].unsqueeze(1).broadcast_to([P, TG * H, NC])).then_inc(c_dve, 1)

            def features(g, h):
                dve.wait_ge(s_exp, H * g + h + 1)
                if not (isinstance(g, int) and g == 0 and h < 4):
                    dve.wait_ge(s_a, H * g + h - 3)
                for j in range(2):
                    last = v.scalar_tensor_tensor(out=phi[:, h % 4, j, :], in0=x_ps[h % 2][:, j, :], scalar=0.0,
                                                  in1=ebuf[:, h % 2, j, :], op0=ALU.max, op1=ALU.add)
                last.then_inc(s_phi, 1)

            def keep_values(g, first):
                dve.wait_ge(s_v, g + 1)
                if not first:
                    dve.wait_ge(s_av, 2 * g)
                v.tensor_tensor(vbd[:, :, :, :, 0:HD].rearrange("p t h c d -> p (t h) c d"),
                                m_ps.rearrange("p (th d) -> p th d", d=HD).unsqueeze(2).broadcast_to([P, TG * H, NC, HD]),
                                blk_mask[:, :, 0:HD].unsqueeze(1).broadcast_to([P, TG * H, NC, HD]),
                                ALU.mult).then_inc(s_vbd, 1)

            def normalise(g, half):
                dve.wait_ge(s_av, 2 * g + half + 1)
                o3 = o_ps.rearrange("p (u w) -> p u w", w=VW)
                v.tensor_scalar(den[:, :], o3[:, :, HD], 1e-8, None, ALU.add).then_inc(s_nrm, 1)
                dve.wait_ge(s_nrm, 2 * (2 * g + half) + 1)
                v.reciprocal(rden[:, :], den[:, :]).then_inc(s_nrm, 1)
                dve.wait_ge(s_nrm, 2 * (2 * g + half) + 2)
                v.tensor_tensor(o_sb[:, :, half, :], o3[:, :, 0:HD], rden[:, :].unsqueeze(2).broadcast_to([P, TG * NC, HD]),
                                ALU.mult).then_inc(s_on, 1)

            def turn_o(g, first):
                dve.wait_ge(s_on, 2 * g + 2)
                if not first:
                    dve.wait_ge(s_y, g)
                v.transpose(oT[:, :, :].rearrange("p t s -> p (t s)"), o_sb[:, :, :, :].rearrange("p u s d -> p (u s d)")).then_inc(s_ot, 1)

            def residual(g):
                dve.wait_ge(s_y, g + 1)
                dve.wait_ge(s_xb, g + 1)
                v.tensor_tensor(x2[:, :, :].rearrange("p t d -> p (t d)"), m_ps, x2[:, :, :].rearrange("p t d -> p (t d)"),
                                ALU.add).then_inc(s_x2, 1)

            def norm2(g):
                dve.wait_ge(s_x2, g + 1)
                for t in range(TG):
                    last = v.bn_stats(ln2_st[:, t, :], x2[:, t, :])
                last.then_inc(s_ln2, 1)
                dve.wait_ge(s_ln2, 3 * g + 1)
                dve.sem_inc(seq_dve, 1)
                for t in range(TG):
                    last = v.bn_aggr(ln2_mv[:, t, :], ln2_st[:, t, :])
                last.then_inc(s_ln2, 1)
                dve.wait_ge(s_ln2, 3 * g + 2)
                v.tensor_scalar(ln2_ve[:, :], ln2_mv[:, :, 1], EPS, None, ALU.add).then_inc(s_ln2, 1)

            def norm2_apply(g, first):
                dve.wait_ge(s_rs2, g + 1)
                for t in range(TG):
                    last = v.tensor_scalar(h2[:, t, :], x2[:, t, :], ln2_mv[:, t, 0:1], ln2_rs[:, t:t + 1],
                                           ALU.subtract, ALU.mult)
                last.then_inc(s_nh, 1)
                dve.wait_ge(s_nh, 2 * g + 1)
                v.tensor_tensor(h2[:, :, :], h2[:, :, :], mod_bc[:, bass.ds(g, 1), 2, :].broadcast_to([P, TG, D]),
                                ALU.mult).then_inc(s_nh, 1)
                dve.wait_ge(s_nh, 2 * g + 2)
                if not first:
                    dve.wait_ge(s_h2t, g)
                    dve.wait_ge(s_rec, g)
                v.tensor_tensor(h2m[:, :, :], h2[:, :, :], mod_bc[:, bass.ds(g, 1), 1, :].broadcast_to([P, TG, D]),
                                ALU.add).then_inc(s_h2, 1)

            def route(g):
                dve.wait_ge(s_lg, g + 1)
                lg = m_ps[:, 0:TG * E].rearrange("p (t e) -> p t e", e=E)
                v.tensor_reduce(top[:, :], lg, AX.X, ALU.max).then_inc(s_rt, 1)
                dve.wait_ge(s_rt, 3 * g + 1)
                v.tensor_tensor(lgd[:, :, :], lg, top[:, :].unsqueeze(2).broadcast_to([P, TG, E]), ALU.subtract).then_inc(s_lgd, 1)
                dve.wait_ge(s_lgd, g + 1)
                v.scalar_tensor_tensor(out=cand[:, :, :], in0=lgd[:, :, :], scalar=0.0,
                                       in1=rev[:, :].unsqueeze(1).broadcast_to([P, TG, E]), op0=ALU.is_ge, op1=ALU.mult).then_inc(s_rt, 1)
                dve.wait_ge(s_rt, 3 * g + 2)
                v.tensor_reduce(cmax[:, :], cand[:, :, :], AX.X, ALU.max).then_inc(s_rt, 1)
                dve.wait_ge(s_rt, 3 * g + 3)
                v.tensor_tensor(pick[:, :, :], cand[:, :, :], cmax[:, :].unsqueeze(2).broadcast_to([P, TG, E]),
                                ALU.is_equal).then_inc(s_pick, 1)

            def gate_score(g, first):
                dve.wait_ge(s_ex, g + 1)
                v.tensor_reduce(lgs[:, :], lge[:, :, :], AX.X, ALU.add).then_inc(s_gs, 1)
                dve.wait_ge(s_gs, g + 1)
                if not first:
                    dve.wait_ge(s_gbs, g)
                v.reciprocal(score[:, :], lgs[:, :]).then_inc(s_sc, 1)

            def position(g, first):
                dve.wait_ge(s_rk, g + 1)
                rk = m_ps[:, 0:TG * E].rearrange("p (t e) -> p t e", e=E)
                ct = m_ps[:, TG * E:2 * TG * E].rearrange("p (t e) -> p t e", e=E)
                n = 7 * g
                v.tensor_copy(pref[:, 0, :], carry[:, :]).then_inc(s_ps, 1)
                for t in range(1, TG):
                    dve.wait_ge(s_ps, n + t)
                    v.tensor_tensor(pref[:, t, :], ct[:, t - 1, :], pref[:, t - 1, :], ALU.add).then_inc(s_ps, 1)
                dve.wait_ge(s_ps, n + TG)
                v.tensor_tensor(carry[:, :], ct[:, TG - 1, :], pref[:, TG - 1, :], ALU.add).then_inc(s_ps, 1)
                v.tensor_tensor(posf[:, :, :], rk, pref[:, :, :], ALU.add).then_inc(s_ps, 1)
                dve.wait_ge(s_ps, n + TG + 2)
                v.tensor_tensor(posf[:, :, :], posf[:, :, :], pick[:, :, :], ALU.mult).then_inc(s_ps, 1)
                dve.wait_ge(s_ps, n + TG + 3)
                v.tensor_reduce(posr[:, :], posf[:, :, :], AX.X, ALU.add).then_inc(s_pr, 1)
                dve.wait_ge(s_pr, g + 1)
                if not first:
                    dve.wait_ge(s_scat, 16 * TG * g)
                v.tensor_copy(pos[:, :], posr[:, :]).then_inc(s_pos, 1)

            def step(g, now, prev, prev2, nxt, first=False, firstp=False, firstp2=False):
                for h in range(H):
                    if h == 0 and nxt:
                        norm1(g + 1, False)
                    if h == 1 and nxt:
                        norm1_apply(g + 1, False)
                    if h == 3 and prev:
                        normalise(g - 1, 1)
                        turn_o(g - 1, firstp)
                    if h == 3 and prev2:
                        route(g - 2)
                    if h == 4 and now:
                        keep_values(g, first)
                    if h == 5 and prev2:
                        gate_score(g - 2, firstp2)
                    if h == 5 and prev:
                        residual(g - 1)
                        norm2(g - 1)
                    if h == 6 and prev:
                        norm2_apply(g - 1, firstp)
                    if h == 7 and prev2:
                        position(g - 2, firstp2)
                    if h == 7 and now:
                        normalise(g, 0)
                    if now:
                        features(g, h)

            step(0, True, False, False, True, first=True)
            step(1, True, True, False, True, firstp=True)
            step(2, True, True, True, True, firstp2=True)
            with dve.Fori(3, NG - 1) as g:
                step(g, True, True, True, True)
            step(NG - 1, True, True, True, False)
            step(NG, False, True, True, False)
            step(NG + 1, False, False, True, False)

            v.tensor_tensor(cnt[:, :], carry[:, :], region0[:, :], ALU.subtract)
            v.tensor_copy(carry_i[:, :], carry[:, :]).then_inc(s_table, 1)
            dve.wait_ge(s_table, 1)
            v.tensor_tensor(full[:, :, :], cnt[:, :].unsqueeze(2).broadcast_to([P, E, NT]),
                            tiles128[:, :].unsqueeze(1).broadcast_to([P, E, NT]), ALU.is_gt).then_inc(s_tab, 1)
            dve.wait_ge(s_tab, 1)
            v.tensor_reduce(nt[:, :], full[:, :, :], AX.X, ALU.add).then_inc(s_tab, 1)
            dve.wait_ge(s_tab, 2)
            v.tensor_scalar(skip[:, :], nt[:, :], -float(P), float(REGION), ALU.mult, ALU.add)
            v.tensor_copy(endt[:, 0, :], nt[:, :]).then_inc(s_tab, 1)
            src, n = 0, 3
            for sh in (1, 2, 4):
                dve.wait_ge(s_tab, n)
                v.tensor_copy(endt[:, 1 - src, 0:sh], endt[:, src, 0:sh])
                v.tensor_tensor(endt[:, 1 - src, sh:E], endt[:, src, sh:E], endt[:, src, 0:E - sh], ALU.add).then_inc(s_tab, 1)
                src, n = 1 - src, n + 1
            dve.wait_ge(s_tab, 6)
            v.tensor_tensor(past[:, :, :], slot_no[:, :].unsqueeze(2).broadcast_to([P, SLOTS, E]),
                            endt[:, src, :].unsqueeze(1).broadcast_to([P, SLOTS, E]), ALU.is_ge).then_inc(s_tab, 1)
            dve.wait_ge(s_tab, 7)
            v.tensor_tensor(hop[:, :, :], past[:, :, :], skip[:, :].unsqueeze(1).broadcast_to([P, SLOTS, E]), ALU.mult)
            v.tensor_reduce(expf[:, 0, :], past[:, :, :], AX.X, ALU.add).then_inc(s_tab, 1)
            dve.wait_ge(s_tab, 8)
            v.tensor_scalar(exp_i[:, :], expf[:, 0, :], float(E - 1), None, ALU.min)
            v.tensor_reduce(rowf[:, 0, :], hop[:, :, :], AX.X, ALU.add).then_inc(s_tab, 1)
            dve.wait_ge(s_tab, 9)
            v.scalar_tensor_tensor(out=rowf[:, 1, :], in0=slot_no[:, :], scalar=float(P), in1=rowf[:, 0, :],
                                   op0=ALU.mult, op1=ALU.add).then_inc(s_tab, 1)
            dve.wait_ge(s_tab, 10)
            v.tensor_scalar(row_i[:, :], rowf[:, 1, :], float(DUMMY), None, ALU.min).then_inc(s_table, 1)
            dve.wait_ge(s_table, 2)

            def expert_of(s):
                return dve.value_load(exp_i[0:1, bass.ds(s, 1)], min_val=0, max_val=E - 1)

            def take_weights(s, b, e):
                if not (isinstance(s, int) and s < 2):
                    dve.wait_ge(f_h, 2 * (s - 1))
                v.tensor_copy(w1_e[:, b % 2, :], w1_sb[:, bass.ds(e * F, F)]).then_inc(f_w, 1)

            def finish(s, b, k, e):
                dve.wait_ge(f_y, s + 1)
                v.tensor_tensor(y1[:, b % 2, :], ps[:, 6 + b % 2, 0:D], b2_bc[:, bass.ds(e * D, D)], ALU.add).then_inc(f_s, 1)
                if not (isinstance(s, int) and s < RING):
                    dve.wait_ge(f_out[b], 16 * k)
                v.tensor_copy(tok[:, b:b + 1], rin[:, b, 3 * D:R])
                dve.wait_ge(f_s, 2 * s + 1)
                v.tensor_tensor(y2[:, b % 2, :], y1[:, b % 2, :], rin[:, b, 2 * D:3 * D], ALU.mult).then_inc(f_s, 1)
                dve.wait_ge(f_s, 2 * s + 2)
                v.tensor_tensor(yo[:, b, :], y2[:, b % 2, :], rin[:, b, D:2 * D], ALU.add).then_inc(f_yd, 1)

            def run(s, b0, n):
                e = [expert_of(s + d) for d in (-2, -1, 0)]
                for d in range(n):
                    b = (b0 + d) % RING
                    take_weights(s + d, b, e[d + 2])
                    if d + 1 < n:
                        e.append(expert_of(s + d + 1))
                    finish(s + d - 2, (b - 2) % RING, (s + d - 2) // RING, e[d])

            dve.wait_ge(l_exp, 64)
            for s in range(2):
                take_weights(s, s, expert_of(s))
            run(2, 2, HEAD - 1)
            with dve.Fori(HEAD + 1, BODY - RING + 2, RING) as s:
                run(s, HEAD + 1, RING)
            run(BODY + 1, (BODY + 1) % RING, SLOTS - BODY - 1)
            for s in range(SLOTS - 2, SLOTS):
                finish(s, s % RING, s // RING, expert_of(s))


_INS = ["L0_attn_x", "L0_attn_w_qkv", "L0_attn_w_out", "L0_attn_b_out", "L0_attn_proj", "L0_ffn_w_red", "L0_ffn_wg",
        "L0_ffn_w1", "L0_ffn_b1", "L0_ffn_w2", "L0_ffn_b2", "L0_c", "L0_wmod"]


def kernel(**inputs):
    import numpy as np
    import concourse.bacc as bacc
    from concourse.bass_utils import run_bass_kernel_spmd

    nc = bacc.Bacc("TRN2", target_bir_lowering=False, num_devices=1)
    arrays, args = {}, []
    for name in _INS:
        a = np.ascontiguousarray(inputs[name])
        if name == "L0_c":
            a = np.ascontiguousarray(a.T)
        if name == "L0_ffn_b1":
            a = np.ascontiguousarray(a.reshape(a.shape[0], -1, P).transpose(2, 0, 1).reshape(P, -1))
        arrays[f"in_{name}"] = a
        args.append(nc.dram_tensor(f"in_{name}", a.shape, mybir.dt.from_np(a.dtype), kind="ExternalInput").ap())
    shape = inputs["L0_attn_x"].shape
    out = nc.dram_tensor("out_0", shape, F32, kind="ExternalOutput").ap()
    adaln_kernel(nc, *args, out)
    r = run_bass_kernel_spmd(nc, [arrays], core_ids=[0])
    return r.results[0]["out_0"]
```

```python
from contextlib import ExitStack

import concourse.bass as bass
from concourse import mybir

P = 128
ALU = mybir.AluOpType
ACT = mybir.ActivationFunctionType
AX = mybir.AxisListType
F32 = mybir.dt.float32
F32R = mybir.dt.float32r
BF16 = mybir.dt.bfloat16
I32 = mybir.dt.int32

EPS = 1e-5


def adaln_kernel(nc, x, w_qkv, w_out, b_out, proj, w_red, wg, w1, b1_t, w2, b2, c_cols, wmod, out):
    B, N, D = x.shape
    H, HD, FEAT = proj.shape
    E, _, F = w1.shape
    GD = w_red.shape[1]
    T = B * N
    NT = T // P
    TG = 4
    GT = TG * P
    NG = T // GT
    GB_ = N // GT
    BLK = 32
    NC = P // BLK
    VW = HD + 1
    HH = H // 2
    FC = F // P
    REGION = T + P
    DUMMY = E * REGION
    SLOTS = NT + E - 1
    RING = 6
    WHOLE = SLOTS // RING * RING
    HEAD = RING - 1
    BODY = HEAD + (SLOTS - 1 - HEAD) // RING * RING
    R = 3 * D + 1
    assert D == P and FEAT == P and H * HD == P and HH == NC and 2 * HD == BLK

    xf = x.rearrange("b n d -> (b n) d")
    of = out.rearrange("b n d -> (b n) d")
    sorted_rows = nc.dram_tensor("sorted_rows", [DUMMY + P, R], F32, kind="Internal").ap()

    ctx = ExitStack()
    with ctx:
        def sb(name, shape, dt=F32):
            return ctx.enter_context(nc.sbuf_tensor(name, shape, dt))

        def sem(name):
            return ctx.enter_context(nc.semaphore(name))

        x_all = sb("x_all", [P, NT, D])
        wqkv_sb = sb("wqkv_sb", [P, 3, D])
        proj_bd = sb("proj_bd", [P, H, FEAT])
        mix_hi = sb("mix_hi", [P, 2, H, FEAT], F32R)
        mix_lo = sb("mix_lo", [P, 2, H, FEAT], F32R)
        wvT = sb("wvT", [P, P])
        wo_sb = sb("wo_sb", [P, P])
        wo_perm = sb("wo_perm", [P, P])
        woT = sb("woT", [P, P])
        wo_g = sb("wo_g", [P, B, P])
        bout_bc = sb("bout_bc", [P, D])
        wmod_sb = sb("wmod_sb", [P, 6 * D])
        cT = sb("cT", [P, B])
        ecT = sb("ecT", [P, B])
        siluT = sb("siluT", [P, B])
        silu_bc = sb("silu_bc", [P, B, P])
        modT = sb("modT", [P, 2, NG])
        mod_bc = sb("mod_bc", [P, B, 4, D])
        signs = sb("signs", [P, B, 2, D])
        mags = sb("mags", [P, B, 2, D])
        wred_sb = sb("wred_sb", [P, GD])
        wredT = sb("wredT", [GD, P])
        wg_sb = sb("wg_sb", [E, GD])
        wg_sq = sb("wg_sq", [E, GD])
        wg_n = sb("wg_n", [E, 4])
        wg_u = sb("wg_u", [E, GD])
        wgT = sb("wgT", [GD, E])
        w_gate = sb("w_gate", [P, E])
        w1b2 = sb("w1b2", [P, E * (F + D)])
        w2_sb = sb("w2_sb", [P, E * FC * D])
        b1_cols = sb("b1_cols", [P, E * FC])
        ident = sb("ident", [P, P])
        before = sb("before", [P, P], BF16)
        ones_b = sb("ones_b", [P, P], BF16)
        blk_mask = sb("blk_mask", [P, NC, VW])
        rev = sb("rev", [P, E])
        ids = sb("ids", [P, NT])
        pad_rec = sb("pad_rec", [P, R])

        ln1_st = sb("ln1_st", [P, TG, 6])
        ln1_mv = sb("ln1_mv", [P, TG, 2])
        ln1_ve = sb("ln1_ve", [P, TG])
        ln2_ve = sb("ln2_ve", [P, TG])
        neg_half = sb("neg_half", [P, TG])
        ln1_rs = sb("ln1_rs", [P, TG])
        xc = sb("xc", [P, TG, D])
        xn = sb("xn", [P, TG, D])
        hT = sb("hT", [P, GT])
        hT_hi = sb("hT_hi", [P, 2, GT], F32R)
        hT_lo = sb("hT_lo", [P, 2, GT], F32R)
        vals = sb("vals", [P, TG, H, HD])
        ebuf = sb("ebuf", [P, 2, 2, GT])
        phi = sb("phi", [P, 4, 2, GT])
        a_sb = sb("a_sb", [P, 2, HH, TG, BLK])
        vbd = sb("vbd", [P, TG, H, NC, VW])
        den = sb("den", [P, TG * NC])
        rden = sb("rden", [P, TG * NC])
        o_sb = sb("o_sb", [P, TG * NC, 2, HD])
        oT = sb("oT", [P, TG, P])
        xb = sb("xb", [P, TG, D])
        x2 = sb("x2", [P, TG, D])
        ln2_st = sb("ln2_st", [P, TG, 6])
        ln2_mv = sb("ln2_mv", [P, TG, 2])
        ln2_rs = sb("ln2_rs", [P, TG])
        h2 = sb("h2", [P, TG, D])
        h2m = sb("h2m", [P, TG, D])
        h2T = sb("h2T", [P, TG, P])
        top = sb("top", [P, TG])
        lgd = sb("lgd", [P, TG, E])
        lge = sb("lge", [P, TG, E])
        lgs = sb("lgs", [P, TG])
        score = sb("score", [P, TG])
        cand = sb("cand", [P, TG, E])
        cmax = sb("cmax", [P, TG])
        pick = sb("pick", [P, TG, E], BF16)
        carry = sb("carry", [P, E])
        posf = sb("posf", [P, TG, E])
        posr3 = sb("posr3", [P, TG, E])
        posr = sb("posr", [P, TG])
        pos = sb("pos", [P, TG], I32)
        lg_sb = sb("lg_sb", [P, TG, E])
        rec = sb("rec", [P, TG, R])
        rec_last = phi[:, :, :, :].rearrange("p a b n -> p (a b n)")[:, 0:TG * R].rearrange("p (t r) -> p t r", t=TG)
        pos_last = sb("pos_last", [P, TG], I32)

        def is_last(g):
            return isinstance(g, int) and g == NG - 1

        def x2_of(g):
            return rec_last[:, :, D:2 * D] if is_last(g) else x2[:, :, :]

        def h2m_of(g):
            return rec_last[:, :, 0:D] if is_last(g) else h2m[:, :, :]

        cnt = sb("cnt", [P, E])
        full = sb("full", [P, E, NT])
        nt = sb("nt", [P, E])
        endt = sb("endt", [P, 2, E])
        skip = sb("skip", [P, E])
        past = sb("past", [P, SLOTS, E])
        hop = sb("hop", [P, SLOTS, E])
        expf = sb("expf", [P, 2, SLOTS])
        rowf = sb("rowf", [P, 2, SLOTS])
        region0 = sb("region0", [P, E])
        tiles128 = sb("tiles128", [P, NT])
        slot_no = sb("slot_no", [P, SLOTS])
        exp_i = sb("exp_i", [P, SLOTS], I32)
        row_i = sb("row_i", [P, SLOTS], I32)
        carry_i = sb("carry_i", [P, E], I32)

        rin = sb("rin", [P, RING, R])
        sT = sb("sT", [P, 2, P])
        flat = (vbd[:, :, :, :, :].rearrange("p t h c w -> p (t h c w)"), ebuf[:, :, :, :].rearrange("p a j n -> p (a j n)"))
        w_slot = [flat[b // 3][:, (b % 3) * (F + D):(b % 3 + 1) * (F + D)] for b in range(RING)]
        gT = sb("gT", [P, 2, FC, P])
        y1 = sb("y1", [P, 2, D])
        y2 = sb("y2", [P, 2, D])
        yo = sb("yo", [P, RING, D])
        tok = sb("tok", [P, RING], I32)

        ps = ctx.enter_context(nc.psum_tensor("ps", [P, 8, 512], F32))
        x_ps = [ps[:, 2 * i:2 * i + 2, :] for i in range(2)]
        a_ps = ps[:, 4, 0:GT // NC]
        t_ps = ps[:, 5, :]
        o_ps = ps[:, 6, 0:TG * NC * VW]
        h_ps = [ps[:, 4 * i:4 * i + 2, :] for i in range(2)]
        m_ps = ps[:, 7, :]

        l_attn = sem("l_attn"); l_mod = sem("l_mod"); l_c = sem("l_c"); l_gate = sem("l_gate"); l_x0 = sem("l_x0"); l_x = sem("l_x")
        l_exp = sem("l_exp")
        c_pool = sem("c_pool"); c_dve = sem("c_dve"); c_mix = sem("c_mix"); c_exp = sem("c_exp"); set_silu = sem("set_silu")
        p_mix = sem("p_mix"); p_cols = sem("p_cols"); p_wv = sem("p_wv"); p_rows = sem("p_rows"); p_turn = sem("p_turn"); p_gate = sem("p_gate")
        set_khi = sem("set_khi"); set_mix = sem("set_mix"); set_cols = sem("set_cols"); set_wv = sem("set_wv"); set_rows = sem("set_rows")
        set_mod = sem("set_mod"); c_mod = sem("c_mod"); set_turn = sem("set_turn"); set_gate = sem("set_gate"); set_wg = sem("set_wg")
        set_perm = sem("set_perm"); c_wg = sem("c_wg"); c_wgr = sem("c_wgr"); set_wog = sem("set_wog"); set_bout = sem("set_bout")
        s_x = sem("s_x"); s_a = sem("s_a"); s_av = sem("s_av"); s_y = sem("s_y"); s_xt = sem("s_xt")
        s_v = sem("s_v"); s_h2t = sem("s_h2t"); s_lg = sem("s_lg"); s_rk = sem("s_rk")
        s_exp = sem("s_exp"); s_asb = sem("s_asb"); s_ht = sem("s_ht"); s_h2ts = sem("s_h2ts"); s_ex = sem("s_ex")
        s_neg = sem("s_neg"); s_xb = sem("s_xb"); s_rec = sem("s_rec"); s_gbs = sem("s_gbs"); s_scat = sem("s_scat")
        s_phi = sem("s_phi"); s_ln1 = sem("s_ln1"); s_xn = sem("s_xn"); s_vbd = sem("s_vbd"); s_nrm = sem("s_nrm")
        s_on = sem("s_on"); s_ot = sem("s_ot"); s_x2 = sem("s_x2"); s_ln2 = sem("s_ln2"); s_h2 = sem("s_h2")
        s_rt = sem("s_rt"); s_pick = sem("s_pick"); s_sc = sem("s_sc"); s_lgd = sem("s_lgd"); s_ps = sem("s_ps"); s_pos = sem("s_pos")
        s_hi = sem("s_hi"); s_lo = sem("s_lo"); s_vs = sem("s_vs"); s_nh = sem("s_nh"); s_lgs = sem("s_lgs"); s_ids = sem("s_ids"); s_xc = sem("s_xc"); s_nm = sem("s_nm"); s_gs = sem("s_gs"); s_pr = sem("s_pr"); f_s = sem("f_s"); seq_pool = sem("seq_pool"); seq_dve = sem("seq_dve"); seq_sp = sem("seq_sp"); s_rs1 = sem("s_rs1"); s_rs2 = sem("s_rs2"); s_tab = sem("s_tab"); s_cr = sem("s_cr"); s_table = sem("s_table"); s_tail = sem("s_tail")
        f_in = [sem(f"f_in{b}") for b in range(RING)]
        f_t = sem("f_t"); f_table = sem("f_table"); f_ts = sem("f_ts"); f_w = sem("f_w"); f_h = sem("f_h"); f_g = sem("f_g")
        f_y = sem("f_y"); f_yd = sem("f_yd");
        f_out = [sem(f"f_out{b}") for b in range(RING)]

        block = ctx.enter_context(nc.Block())

        def pad_region(eng, e):
            row = eng.value_load(carry_i[0:1, e:e + 1], min_val=e * REGION, max_val=e * REGION + T)
            eng.dma_start(sorted_rows[bass.ds(row, P), :], pad_rec[:, :]).then_inc(s_tail, 16)

        @block.sync
        def _(sp):
            sp.dma_start(wqkv_sb[:, :, :], w_qkv.rearrange("(j r) d -> r j d", j=3)).then_inc(l_attn, 16)
            sp.dma_start(proj_bd[:, 0, :], proj.rearrange("h k f -> (h k) f")).then_inc(l_attn, 16)
            xt = xf.rearrange("(t p) d -> p t d", p=P)
            sp.dma_start(x_all[:, 0:TG, :], xt[:, 0:TG, :]).then_inc(l_x0, 16)
            sp.dma_start(cT[:, :], c_cols).then_inc(l_c, 16)
            sp.dma_start(wmod_sb[:, :], wmod).then_inc(l_mod, 16)
            sp.dma_start(wo_sb[:, :], w_out).then_inc(l_gate, 16)
            sp.dma_start(bout_bc[:, :], b_out.rearrange("(a d) -> a d", a=1).partition_broadcast(P)).then_inc(l_gate, 16)
            sp.dma_start(wred_sb[:, :], w_red).then_inc(l_gate, 16)
            sp.dma_start(wg_sb[:, :], wg).then_inc(l_gate, 16)
            sp.dma_start(x_all[:, TG:NT, :], xt[:, TG:NT, :]).then_inc(l_x, 16)
            by_expert = w1b2[:, :].rearrange("p (e f) -> p e f", e=E)
            sp.dma_start(by_expert[:, :, 0:F], w1.rearrange("e d f -> d e f")).then_inc(l_exp, 16)
            sp.dma_start(w2_sb[:, :].rearrange("p (e c d) -> p e c d", e=E, c=FC),
                         w2.rearrange("e (c p) d -> p e c d", p=P)).then_inc(l_exp, 16)
            sp.dma_start(b1_cols[:, :], b1_t).then_inc(l_exp, 16)
            sp.dma_start(by_expert[:, :, F:F + D], b2.rearrange("(a e) f -> a e f", a=1).partition_broadcast(P)).then_inc(l_exp, 16)
            sp.wait_ge(c_dve, 1)
            sp.dma_start(sorted_rows[DUMMY:DUMMY + P, :], pad_rec[:, :]).then_inc(s_tail, 16)
            def copy_record(g, first):
                sp.wait_ge(s_h2, g + 1)
                sp.sem_inc(seq_sp, 1)
                if not first:
                    sp.wait_ge(s_scat, 16 * TG * g)
                sp.dma_start(rec[:, :, 0:D], h2m[:, :, :]).then_inc(s_rec, 16)
                sp.dma_start(rec[:, :, D:2 * D], x2[:, :, :]).then_inc(s_rec, 16)

            copy_record(0, True)
            with sp.Fori(1, NG - 1) as g:
                copy_record(g, False)
            sp.wait_ge(s_table, 1)
            for e in range(E // 2):
                pad_region(sp, e)
            sp.wait_ge(s_table, 2)
            first_rows = [sp.value_load(row_i[0:1, s:s + 1], min_val=0, max_val=DUMMY) for s in range(RING)]
            sp.wait_ge(s_tail, 16 * (E + 1))
            sp.wait_ge(s_scat, 16 * NT)

            def load_slot(s, b):
                row = sp.value_load(row_i[0:1, bass.ds(s, 1)], min_val=0, max_val=DUMMY)
                sp.dma_start(rin[:, b, :], sorted_rows[bass.ds(row, P), :]).then_inc(f_in[b], 16)

            def reload_slot(s, b):
                sp.wait_ge(f_yd, s - RING + 1)
                load_slot(s, b)

            for s, row in enumerate(first_rows):
                sp.dma_start(rin[:, s, :], sorted_rows[bass.ds(row, P), :]).then_inc(f_in[s], 16)
            with sp.Fori(RING, WHOLE - RING + 1, RING) as s:
                for b in range(RING):
                    reload_slot(s + b, b)
            for s in range(WHOLE, SLOTS):
                reload_slot(s, s % RING)

        @block.gpsimd
        def _(pool):
            g_ = nc.gpsimd
            g_.memset(ident[:, :], 0.0).then_inc(c_pool, 1)
            g_.memset(ones_b[:, :], 1.0).then_inc(c_pool, 1)
            g_.memset(blk_mask[:, :, :], 1.0).then_inc(c_pool, 1)
            g_.memset(neg_half[:, :], -0.5)
            g_.iota(tiles128[:, :], [[P, NT]], base=0, channel_multiplier=0, allow_small_or_imprecise_dtypes=True)
            g_.iota(region0[:, :], [[REGION, E]], base=0, channel_multiplier=0, allow_small_or_imprecise_dtypes=True)
            g_.iota(slot_no[:, :], [[1, SLOTS]], base=0, channel_multiplier=0, allow_small_or_imprecise_dtypes=True)
            g_.iota(rev[:, :], [[-1, E]], base=E, channel_multiplier=0, allow_small_or_imprecise_dtypes=True)
            g_.iota(ids[:, :], [[P, NT]], base=0, channel_multiplier=1,
                    allow_small_or_imprecise_dtypes=True).then_inc(c_pool, 1)
            pool.wait_ge(c_pool, 4)
            g_.affine_select(out=ident[:, :], in_=ident[:, :], compare_op=ALU.not_equal, fill=1.0,
                             base=0, pattern=[[-1, P]], channel_multiplier=1).then_inc(c_pool, 1)
            g_.affine_select(out=before[:, :], in_=ones_b[:, :], compare_op=ALU.is_gt, fill=0.0,
                             base=0, pattern=[[1, P]], channel_multiplier=-1).then_inc(c_pool, 1)
            g_.affine_select(out=blk_mask[:, :, :], in_=blk_mask[:, :, :], compare_op=ALU.is_ge, fill=0.0,
                             base=0, pattern=[[-BLK, NC], [0, VW]], channel_multiplier=1).then_inc(c_pool, 1)
            pool.wait_ge(c_pool, 7)
            g_.affine_select(out=blk_mask[:, :, :], in_=blk_mask[:, :, :], compare_op=ALU.is_ge, fill=0.0,
                             base=BLK - 1, pattern=[[BLK, NC], [0, VW]], channel_multiplier=-1).then_inc(c_pool, 1)
            pool.wait_ge(l_attn, 32)
            g_.affine_select(out=proj_bd[:, 1:H, :], in_=proj_bd[:, 0:1, :].broadcast_to([P, H - 1, FEAT]),
                             compare_op=ALU.is_ge, fill=0.0, base=-HD,
                             pattern=[[-HD, H - 1], [0, FEAT]], channel_multiplier=1).then_inc(c_pool, 1)
            pool.wait_ge(c_pool, 9)
            g_.affine_select(out=proj_bd[:, :, :], in_=proj_bd[:, :, :], compare_op=ALU.is_ge, fill=0.0,
                             base=HD - 1, pattern=[[HD, H], [0, FEAT]], channel_multiplier=-1).then_inc(c_pool, 1)

            def rsqrt(out, in_, done):
                n = in_.shape[0]
                g_.tensor_tensor(out, in_, neg_half[0:n, 0:in_.shape[1]], ALU.pow).then_inc(done, 1)

            def norm1_apply(g):
                pool.wait_ge(l_x, 16)
                pool.wait_ge(s_ln1, 3 * g + 3)
                rsqrt(ln1_rs[:, :], ln1_ve[:, :], s_rs1)
                g_.tensor_tensor(xc[:, :, :], x_all[:, bass.ds(g * TG, TG), :], ln1_mv[:, :, 0:1].broadcast_to([P, TG, D]),
                                 ALU.subtract).then_inc(s_xc, 1)
                pool.wait_ge(s_rs1, g + 1)
                pool.wait_ge(s_xc, g)
                pool.wait_ge(s_xt, g)
                g_.tensor_tensor(xn[:, :, :], xc[:, :, :], ln1_rs[:, :].unsqueeze(2).broadcast_to([P, TG, D]),
                                 ALU.mult).then_inc(s_xn, 1)

            pool.wait_ge(s_ln1, 3)
            rsqrt(ln1_rs[:, :], ln1_ve[:, :], s_rs1)

            def setup_rows():
                pool.wait_ge(set_mod, 1)
                pool.wait_ge(set_turn, 1)
                g_.tensor_tensor(wo_g[:, :, :], woT[:, :].unsqueeze(1).broadcast_to([P, B, P]), mod_bc[:, :, 0, :],
                                 ALU.mult).then_inc(set_wog, 1)
                pool.wait_ge(set_wog, 1)
                pool.wait_ge(l_gate, 64)
                g_.tensor_tensor(mod_bc[:, :, 0, :], mod_bc[:, :, 0, :],
                                 bout_bc[:, :].unsqueeze(1).broadcast_to([P, B, D]), ALU.mult).then_inc(set_bout, 1)

            def wait_then(s, value):
                pool.wait_ge(s, value)
                pool.sem_inc(seq_pool, 1)

            def residual_base(g, first):
                pool.wait_ge(l_x, 16)
                pool.wait_ge(l_x0, 16)
                pool.wait_ge(set_bout, 1)
                if not first:
                    pool.wait_ge(s_x2, g)
                g_.tensor_tensor(xb[:, :, :], x_all[:, bass.ds(g * TG, TG), :],
                                 mod_bc[:, bass.ds(g // GB_, 1), 0, :].broadcast_to([P, TG, D]), ALU.add).then_inc(s_xb, 1)

            def split_lo(g):
                pool.wait_ge(s_hi, g + 1)
                g_.tensor_tensor(hT_lo[:, bass.ds(g % 2, 1), :].rearrange("p a n -> p (a n)"), hT[:, :],
                                 hT_hi[:, bass.ds(g % 2, 1), :].rearrange("p a n -> p (a n)").bitcast(F32), ALU.subtract).then_inc(s_lo, 1)

            def norm2_scale(g, first):
                pool.wait_ge(s_rs2, g + 1)
                pool.wait_ge(s_nh, g + 1)
                g_.tensor_tensor(h2[:, :, :], h2[:, :, :], ln2_rs[:, :].unsqueeze(2).broadcast_to([P, TG, D]), ALU.mult).then_inc(s_nm, 1)
                pool.wait_ge(s_nm, g + 1)
                if not first:
                    pool.wait_ge(s_h2t, g)
                    pool.wait_ge(s_rec, 32 * g)
                g_.tensor_tensor(h2m[:, :, :], h2[:, :, :], mod_bc[:, bass.ds(g // GB_, 1), 1, :].broadcast_to([P, TG, D]),
                                 ALU.add).then_inc(s_h2, 1)

            def build_scale(g, first):
                pool.wait_ge(s_sc, g + 1)
                if not first and not is_last(g):
                    wait_then(s_scat, 16 * TG * g)
                if is_last(g):
                    pool.wait_ge(s_h2, NG)
                to = rec_last if is_last(g) else rec
                g_.tensor_copy(to[:, :, 3 * D:3 * D + 1], ids[:, bass.ds(g * TG, TG)].unsqueeze(2)).then_inc(s_ids, 1)
                g_.tensor_tensor(to[:, :, 2 * D:3 * D], mod_bc[:, bass.ds(g // GB_, 1), 3, :].broadcast_to([P, TG, D]),
                                 score[:, :].unsqueeze(2).broadcast_to([P, TG, D]), ALU.mult).then_inc(s_gbs, 1)

            def scatter(g):
                pool.wait_ge(s_pos, g + 1)
                pool.wait_ge(s_gbs, g + 1)
                pool.wait_ge(s_ids, g + 1)
                if is_last(g):
                    pool.wait_ge(s_h2, NG)
                else:
                    wait_then(s_rec, 32 * (g + 1))
                rows, rows_at = (rec_last, pos_last) if is_last(g) else (rec, pos)
                for t in range(TG):
                    g_.indirect_dma_start(out=sorted_rows[:, :],
                                          out_offset=bass.IndirectOffsetOnAxis(ap=rows_at[:, t:t + 1], axis=0),
                                          in_=rows[:, t, :], in_offset=None).then_inc(s_scat, 16)

            def step(g, nxt=False, prev=False, prev2=False, prev3=False, firstp=False, firstp2=False):
                if prev2:
                    norm2_scale(g - 2, firstp2)
                if prev3:
                    scatter(g - 3)
                if prev:
                    residual_base(g - 1, firstp)
                if nxt:
                    norm1_apply(g + 1)
                if isinstance(g, int) and g == 0:
                    pool.wait_ge(c_wg, 3)
                    rsqrt(wg_n[:, 2:3], wg_n[:, 1:2], c_wgr)
                if nxt:
                    split_lo(g + 1)
                if isinstance(g, int) and g == 0:
                    setup_rows()
                if prev2:
                    build_scale(g - 2, firstp2)
                if prev:
                    pool.wait_ge(s_ln2, 3 * g)
                    rsqrt(ln2_rs[:, :], ln2_ve[:, :], s_rs2)

            split_lo(0)
            step(0, nxt=True)
            step(1, nxt=True, prev=True, firstp=True)
            step(2, nxt=True, prev=True, prev2=True, firstp2=True)
            step(3, nxt=True, prev=True, prev2=True, prev3=True)
            with pool.Fori(4, NG - 1) as g:
                step(g, nxt=True, prev=True, prev2=True, prev3=True)
            step(NG - 1, prev=True, prev2=True, prev3=True)

            norm2_scale(NG - 2, False)
            residual_base(NG - 1, False)
            scatter(NG - 3)
            pool.wait_ge(s_ln2, 3 * NG)
            rsqrt(ln2_rs[:, :], ln2_ve[:, :], s_rs2)
            build_scale(NG - 2, False)
            scatter(NG - 2)
            build_scale(NG - 1, False)
            scatter(NG - 1)

            def put(s, b):
                wait_then(f_yd, s + 1)
                g_.indirect_dma_start(out=of[:, :], out_offset=bass.IndirectOffsetOnAxis(ap=tok[:, b:b + 1], axis=0),
                                      in_=yo[:, b, :], in_offset=None, bounds_check=T - 1,
                                      oob_is_err=False).then_inc(f_out[b], 16)

            with pool.Fori(0, WHOLE - RING + 1, RING) as s:
                for b in range(RING):
                    put(s + b, b)
            for s in range(WHOLE, SLOTS):
                put(s, s % RING)
            for b in range(RING):
                pool.wait_ge(f_out[b], 16 * ((SLOTS - b + RING - 1) // RING))

        @block.scalar
        def _(act):
            act.wait_ge(l_c, 16)
            nc.scalar.activation(ecT[:, :], cT[:, :], ACT.Exp, scale=-1.0).then_inc(c_exp, 1)

            def keep_mix_k(i):
                act.wait_ge(p_mix, 2 * i + 2)
                nc.scalar.copy(mix_hi[:, 1, 4 * i:4 * i + 4, :].rearrange("p h f -> p (h f)"), ps[:, 2 * i + 1, :]).then_inc(set_khi, 1)

            def exp_head(g, h, between):
                act.wait_ge(s_x, 2 * (H * g + h + 1))
                if not (isinstance(g, int) and g == 0 and h < 2):
                    act.wait_ge(s_phi, 2 * (H * g + h - 1))
                nc.scalar.activation(ebuf[:, h % 2, :, :], x_ps[h % 2], ACT.Relu, scale=-1.0).then_inc(s_neg, 1)
                between()
                act.wait_ge(s_neg, H * g + h + 1)
                for j in range(2):
                    nc.scalar.activation(ebuf[:, h % 2, j, :], ebuf[:, h % 2, j, :], ACT.Exp, scale=-1.0).then_inc(s_exp, 1)

            def keep_a(g, h, first):
                act.wait_ge(s_a, H * g + h + 1)
                if h % HH == 0 and not first:
                    act.wait_ge(s_av, 2 * g + h // HH - 1)
                nc.scalar.copy(a_sb[:, h // HH, h % HH, :, :], a_ps.rearrange("p (t s) -> p t s", t=TG)).then_inc(s_asb, 1)

            def keep_hT(g, first):
                act.wait_ge(s_xt, g + 1)
                if first:
                    act.wait_ge(set_cols, 1)
                else:
                    act.wait_ge(s_v, g)
                    act.wait_ge(s_lo, g)
                nc.scalar.activation(hT[:, :], t_ps, ACT.Identity, bias=modT[:, 0, bass.ds(g, 1)],
                                     scale=modT[:, 1, bass.ds(g, 1)]).then_inc(s_ht, 1)

            def keep_v(g, first):
                act.wait_ge(s_v, g + 1)
                if not first:
                    act.wait_ge(s_vbd, g)
                nc.scalar.copy(vals[:, :, :, :].rearrange("p t h d -> p (t h d)"), t_ps).then_inc(s_vs, 1)

            def keep_h2T(g):
                act.wait_ge(s_h2t, g + 1)
                nc.scalar.copy(h2T[:, :, :].rearrange("p t d -> p (t d)"), t_ps if is_last(g) else m_ps).then_inc(s_h2ts, 1)

            def keep_logits(g):
                act.wait_ge(s_lg, g + 1)
                nc.scalar.copy(lg_sb[:, :, :].rearrange("p t e -> p (t e)"), (ps[:, 6, :] if is_last(g) else m_ps)[:, 0:TG * E]).then_inc(s_lgs, 1)

            def gate_exp(g):
                act.wait_ge(s_lgd, g + 1)
                nc.scalar.activation(lge[:, :, :], lgd[:, :, :], ACT.Exp).then_inc(s_ex, 1)

            def step(g, now, prev, prev2, nxt, first=False, first2=False):
                for h in range(H):
                    def older():
                        if h < 2 and prev:
                            keep_a(g - 1, h + 6, first2)
                        if h >= 2 and now:
                            keep_a(g, h - 2, first)

                    if h == 3 and prev2:
                        keep_h2T(g - 2)
                    if h == 4 and prev2:
                        keep_logits(g - 2)
                    if now:
                        exp_head(g, h, older)
                    else:
                        older()
                    if h == 0 and now:
                        keep_v(g, first)
                    if h == 5 and prev2:
                        gate_exp(g - 2)
                    if h == 5 and nxt:
                        keep_hT(g + 1, False)

            keep_mix_k(0)
            keep_hT(0, True)
            keep_mix_k(1)
            step(0, True, False, False, True, first=True)
            step(1, True, True, False, True, first2=True)
            with act.Fori(2, NG - 1) as g:
                step(g, True, True, True, True)
            step(NG - 1, True, True, True, False)

            keep_a(NG - 1, H - 2, False)
            keep_a(NG - 1, H - 1, False)
            for g in (NG - 2, NG - 1):
                keep_h2T(g)
                keep_logits(g)
                gate_exp(g)

            act.wait_ge(s_table, 1)
            for e in range(E // 2, E):
                pad_region(act, e)
            nc.scalar.activation(lge[:, 0, 0:1], neg_half[:, 0:1], ACT.Gelu).then_inc(f_table, 1)


            def keep_in(s, b):
                act.wait_ge(f_t, s + 1)
                nc.scalar.copy(sT[:, b, :], ps[:, 2 + b, 0:P]).then_inc(f_ts, 1)

            def gelu(s, b):
                e = act.value_load(exp_i[0:1, bass.ds(s, 1)], min_val=0, max_val=E - 1)
                for j in range(FC // 2):
                    act.wait_ge(f_h, 2 * s + j + 1)
                    for i in range(2):
                        c_ = 2 * j + i
                        last = nc.scalar.activation(gT[:, b, c_, :], h_ps[b][:, j, i * P:(i + 1) * P], ACT.Gelu,
                                                    bias=b1_cols[:, bass.ds(e * FC + c_, 1)])
                last.then_inc(f_g, 1)

            act.wait_ge(s_table, 2)
            act.wait_ge(l_exp, 64)
            keep_in(0, 0)
            with act.Fori(0, WHOLE - RING + 1, RING) as s:
                for b in range(RING):
                    keep_in(s + b + 1, (b + 1) % 2)
                    gelu(s + b, b % 2)
            for s in range(WHOLE, SLOTS):
                if s + 1 < SLOTS:
                    keep_in(s + 1, (s + 1) % 2)
                gelu(s, s % 2)

        @block.tensor
        def _(pe):
            mm = nc.tensor.matmul
            def keep_busy(n, bank):
                for _ in range(n):
                    mm(bank, ones_b[:, :], ones_b[:, :].unsqueeze(1).broadcast_to([P, 4, P]), start=True, stop=True)

            pe.wait_ge(c_pool, 2)
            keep_busy(11, m_ps)
            pe.wait_ge(c_pool, 10)
            pe.wait_ge(l_attn, 32)

            def fold(j, i):
                mm(ps[:, 2 * i + j, :], wqkv_sb[:, j, :], proj_bd[:, 4 * i:4 * i + 4, :].rearrange("p h f -> p (h f)"),
                   start=True, stop=True).then_inc(p_mix, 1)

            def turn_xn(g, first):
                pe.wait_ge(s_xn, g + 1)
                if not first:
                    pe.wait_ge(s_vs, g)
                for t in range(TG):
                    last = nc.tensor.transpose(t_ps[:, t * P:(t + 1) * P], xn[:, t, :], ident[:, :])
                last.then_inc(s_xt, 1)

            fold(0, 0)
            fold(1, 0)
            pe.wait_ge(set_silu, 1)
            pe.wait_ge(l_mod, 16)
            for j in range(2):
                last = mm(ps[:, 6, 8 * j:8 * j + B], wmod_sb[:, j * D:(j + 1) * D], siluT[:, :], start=True, stop=True)
            last.then_inc(p_cols, 1)
            turn_xn(0, True)
            fold(0, 1)
            fold(1, 1)
            nc.tensor.transpose(ps[:, 4, 0:P], wqkv_sb[:, 2, :], ident[:, :]).then_inc(p_wv, 1)

            def setup_rows(b):
                if b == 0:
                    pe.wait_ge(set_silu, 2)
                else:
                    pe.wait_ge(set_rows, b)
                mm(m_ps, silu_bc[:, b, :], wmod_sb[:, 2 * D:6 * D], start=True, stop=True).then_inc(p_rows, 1)

            def setup_turns():
                pe.wait_ge(set_perm, 1)
                pe.wait_ge(l_gate, 64)
                nc.tensor.transpose(ps[:, 6, 0:P], wo_perm[:, :], ident[:, :])
                nc.tensor.transpose(ps[0:GD, 6, P:2 * P], wred_sb[:, :], ident[:, :])
                pe.wait_ge(set_wg, 1)
                nc.tensor.transpose(ps[0:GD, 6, 2 * P:2 * P + E], wg_u[:, :], ident[0:E, 0:E]).then_inc(p_turn, 1)

            def setup_gate():
                pe.wait_ge(set_turn, 1)
                mm(ps[:, 6, 0:E], wredT[:, :], wgT[:, :], start=True, stop=True).then_inc(p_gate, 1)

            def feats(g, h):
                if h == 0:
                    pe.wait_ge(s_lo, g + 1)
                if isinstance(g, int) and g == 0 and h < 2:
                    pe.wait_ge(set_mix, h + 1)
                hi, lo = (part[:, bass.ds(g % 2, 1), :].rearrange("p a n -> p (a n)") for part in (hT_hi, hT_lo))
                for j in range(2):
                    if not (isinstance(g, int) and g == 0 and h < 2):
                        pe.wait_ge(s_phi, 2 * (H * g + h) - 3 + j)
                    mm(x_ps[h % 2][:, j, :], mix_lo[:, j, h, :], hi, start=True, stop=False)
                    mm(x_ps[h % 2][:, j, :], mix_hi[:, j, h, :], lo, start=False, stop=False)
                    mm(x_ps[h % 2][:, j, :], mix_hi[:, j, h, :], hi, start=False, stop=True).then_inc(s_x, 1)

            def scores(g, h):
                pe.wait_ge(s_phi, 2 * (H * g + h + 1))
                if not (isinstance(g, int) and g == 0 and h == 0):
                    pe.wait_ge(s_asb, H * g + h)
                for t in range(TG):
                    for c_ in range(NC):
                        at = t * P + c_ * BLK
                        last = mm(a_ps[c_ * BLK:(c_ + 1) * BLK, t * BLK:(t + 1) * BLK],
                                  phi[:, h % 4, 1, at:at + BLK], phi[:, h % 4, 0, at:at + BLK], start=True, stop=True)
                last.then_inc(s_a, 1)

            def apply_values(g, half, first):
                pe.wait_ge(s_asb, H * g + HH * (half + 1))
                pe.wait_ge(s_vbd, g + 1)
                if not first:
                    pe.wait_ge(s_on, 2 * g + half)
                for t in range(TG):
                    for q in range(HH):
                        last = mm(o_ps[q * BLK:(q + 1) * BLK, t * NC * VW:(t + 1) * NC * VW], a_sb[:, half, q, t, :],
                                  vbd[:, t, half * HH + q, :, :].rearrange("p c d -> p (c d)"), start=True, stop=True)
                last.then_inc(s_av, 1)

            def project_out(g, bank=m_ps):
                pe.wait_ge(s_ot, g + 1)
                pe.wait_ge(set_wog, 1)
                for t in range(TG):
                    last = mm(bank[:, t * P:(t + 1) * P], oT[:, t, :], wo_g[:, bass.ds(g // GB_, 1), :].rearrange("p a d -> p (a d)"),
                              start=True, stop=True)
                last.then_inc(s_y, 1)

            def values(g):
                if isinstance(g, int) and g == 0:
                    pe.wait_ge(set_wv, 1)
                pe.wait_ge(s_ht, g + 1)
                for t in range(TG):
                    last = mm(t_ps[:, t * P:(t + 1) * P], hT[:, t * P:(t + 1) * P], wvT[:, :], start=True, stop=True)
                last.then_inc(s_v, 1)

            def turn_h2(g, bank=m_ps):
                pe.wait_ge(s_h2, g + 1)
                for t in range(TG):
                    last = nc.tensor.transpose(bank[:, t * P:(t + 1) * P], h2m_of(g)[:, t, :], ident[:, :])
                last.then_inc(s_h2t, 1)

            def gate(g, bank=m_ps):
                pe.wait_ge(s_h2ts, g + 1)
                for t in range(TG):
                    last = mm(bank[:, t * E:(t + 1) * E], h2T[:, t, :], w_gate[:, :], start=True, stop=True)
                last.then_inc(s_lg, 1)

            def rank(g):
                pe.wait_ge(s_pick, g + 1)
                for t in range(TG):
                    for u in range(t + 1):
                        mm(m_ps[:, t * E:(t + 1) * E], before[:, :] if u == t else ones_b[:, :], pick[:, u, :],
                           start=(u == 0), stop=(u == t))
                for t in range(TG):
                    last = mm(m_ps[:, TG * E:(TG + 1) * E], ones_b[:, :], pick[:, t, :], start=(t == 0), stop=(t == TG - 1))
                last.then_inc(s_rk, 1)

            def step(g, prev, prev2, nxt):
                for h in range(H):
                    feats(g, h)
                    if h == 0:
                        values(g)
                    if h == 3 and prev2:
                        gate(g - 2)
                    if h == 5 and prev:
                        if prev2:
                            pe.wait_ge(s_lgs, g - 1)
                        project_out(g - 1)
                    if h == 7 and prev2:
                        pe.wait_ge(s_x2, g)
                        rank(g - 2)
                    if h < 2 and prev:
                        scores(g - 1, h + 6)
                    if h >= 2:
                        scores(g, h - 2)
                    if isinstance(g, int) and g == 0:
                        if h < B:
                            setup_rows(h)
                        if h == 5:
                            setup_turns()
                        if h == 7:
                            setup_gate()
                    if h == 0 and prev:
                        if isinstance(g, int) and g == 1:
                            pe.wait_ge(set_gate, 1)
                        apply_values(g - 1, 0, isinstance(g, int) and g == 1)
                    if h == 2 and prev2:
                        pe.wait_ge(s_x2, g - 1)
                        turn_h2(g - 2)
                    if h == 2 and prev:
                        apply_values(g - 1, 1, False)
                    if h == 5 and nxt:
                        turn_xn(g + 1, False)

            step(0, False, False, True)
            step(1, True, False, True)
            with pe.Fori(2, NG - 1) as g:
                step(g, True, True, True)
            step(NG - 1, True, True, False)

            for half in range(2):
                scores(NG - 1, H - 2 + half)
                keep_busy(5, x_ps[0][:, 0, :])
                apply_values(NG - 1, half, False)
            pe.wait_ge(s_pos, NG - 2)
            turn_h2(NG - 2)
            keep_busy(4, x_ps[0][:, 0, :])
            project_out(NG - 1, t_ps)
            gate(NG - 2)
            pe.wait_ge(s_lgs, NG - 1)
            rank(NG - 2)
            keep_busy(8, x_ps[0][:, 0, :])
            pe.wait_ge(s_x2, NG)
            turn_h2(NG - 1, t_ps)
            gate(NG - 1, ps[:, 6, :])
            pe.wait_ge(s_pos, NG - 1)
            rank(NG - 1)

            def turn_in(s, b, k):
                pe.wait_ge(f_in[b], 16 * (k + 1))
                nc.tensor.transpose(ps[:, 2 + b % 2, 0:P], rin[:, b, 0:D], ident[:, :]).then_inc(f_t, 1)

            def hidden(s, b):
                pe.wait_ge(f_w, s + 1)
                pe.wait_ge(f_ts, s + 1)
                for j in range(FC // 2):
                    for i in range(2):
                        c_ = 2 * j + i
                        last = mm(h_ps[b % 2][:, j, i * P:(i + 1) * P], w_slot[b][:, c_ * P:(c_ + 1) * P], sT[:, b % 2, :],
                                  start=True, stop=True)
                    last.then_inc(f_h, 1)

            def expert_of(s):
                return pe.value_load(exp_i[0:1, bass.ds(s, 1)], min_val=0, max_val=E - 1)

            def outer(s, b, e):
                if not (isinstance(s, int) and s < 2):
                    pe.wait_ge(f_s, 2 * (s - 2) + 1)
                pe.wait_ge(f_g, s + 1)
                for c_ in range(FC):
                    last = mm(ps[:, 6 + b % 2, 0:D], gT[:, b % 2, c_, :], w2_sb[:, bass.ds(e * (FC * D) + c_ * D, D)],
                              start=(c_ == 0), stop=(c_ == FC - 1))
                last.then_inc(f_y, 1)

            keep_busy(22, x_ps[0][:, 0, :])
            pe.wait_ge(s_table, 2)
            pe.wait_ge(l_exp, 64)
            pe.wait_ge(s_pos, NG)
            keep_busy(24, x_ps[0][:, 0, :])
            turn_in(0, 0, 0)
            turn_in(1, 1, 0)
            hidden(0, 0)

            def pipe(s, b, k):
                e = expert_of(s - 1)
                turn_in(s + 1, (b + 1) % RING, k)
                hidden(s, b)
                outer(s - 1, (b - 1) % RING, e)

            for s in range(1, HEAD):
                pipe(s, s % RING, (s + 1) // RING)
            with pe.Fori(HEAD, BODY - RING + 1, RING) as s:
                for d in range(RING):
                    pipe(s + d, (HEAD + d) % RING, (s + d + 1) // RING)
            for s in range(BODY, SLOTS - 1):
                pipe(s, s % RING, (s + 1) // RING)
            hidden(SLOTS - 1, (SLOTS - 1) % RING)
            outer(SLOTS - 2, (SLOTS - 2) % RING, expert_of(SLOTS - 2))
            outer(SLOTS - 1, (SLOTS - 1) % RING, expert_of(SLOTS - 1))

        @block.vector
        def _(dve):
            v = nc.vector
            v.memset(pad_rec[:, 0:3 * D], 0.0)
            v.memset(pad_rec[:, 3 * D:R], float(T)).then_inc(c_dve, 1)
            def norm1_stats(g, tiles, first):
                if first:
                    dve.wait_ge(l_x0, 16)
                else:
                    dve.wait_ge(l_x, 16)
                for t in tiles:
                    last = v.bn_stats(ln1_st[:, t, :], x_all[:, bass.ds(g * TG + t, 1), :].rearrange("p a d -> p (a d)"))
                if TG - 1 in tiles:
                    last.then_inc(s_ln1, 1)

            def norm1_moments(g):
                dve.wait_ge(s_ln1, 3 * g + 1)
                dve.sem_inc(seq_dve, 1)
                for t in range(TG):
                    last = v.bn_aggr(ln1_mv[:, t, :], ln1_st[:, t, :])
                last.then_inc(s_ln1, 1)

            def norm1_variance(g):
                dve.wait_ge(s_ln1, 3 * g + 2)
                v.tensor_scalar(ln1_ve[:, :], ln1_mv[:, :, 1], EPS, None, ALU.add).then_inc(s_ln1, 1)

            def split_hi(g):
                dve.wait_ge(s_ht, g + 1)
                if not (isinstance(g, int) and g < 2):
                    dve.wait_ge(s_x, 2 * H * (g - 1))
                v.tensor_copy(hT_hi[:, bass.ds(g % 2, 1), :].rearrange("p a n -> p (a n)"), hT[:, :]).then_inc(s_hi, 1)

            norm1_stats(0, range(TG), True)
            norm1_moments(0)
            norm1_variance(0)
            dve.wait_ge(c_exp, 1)
            v.tensor_scalar(ecT[:, :], ecT[:, :], 1.0, None, ALU.add).then_inc(c_dve, 1)
            dve.wait_ge(c_dve, 2)
            v.reciprocal(ecT[:, :], ecT[:, :]).then_inc(c_dve, 1)
            dve.wait_ge(c_dve, 3)
            v.tensor_tensor(siluT[:, :], cT[:, :], ecT[:, :], ALU.mult).then_inc(set_silu, 1)
            dve.wait_ge(s_rs1, 1)
            for t in range(TG):
                last = v.tensor_scalar(xn[:, t, :], x_all[:, t, :], ln1_mv[:, t, 0:1], ln1_rs[:, t:t + 1], ALU.subtract, ALU.mult)
            last.then_inc(s_xn, 1)

            def split_mix(j, i, part):
                at = slice(4 * i, 4 * i + 4)
                hi, lo = (m[:, j, at, :].rearrange("p h f -> p (h f)") for m in (mix_hi, mix_lo))
                if part == "hi":
                    return v.tensor_copy(hi, ps[:, 2 * i + j, :])
                return v.tensor_tensor(lo, ps[:, 2 * i + j, :], hi.bitcast(F32), ALU.subtract)

            for i in range(2):
                dve.wait_ge(p_mix, 2 * i + 1)
                split_mix(0, i, "hi").then_inc(c_mix, 1)
                dve.wait_ge(c_mix, i + 1)
                split_mix(0, i, "lo")
                if i == 0:
                    dve.wait_ge(p_cols, 1)
                    v.tensor_copy(modT[:, 0, :].rearrange("p (b r) -> p b r", b=B), ps[:, 6, 0:B].unsqueeze(2).broadcast_to([P, B, GB_]))
                    v.tensor_scalar(modT[:, 1, :].rearrange("p (b r) -> p b r", b=B), ps[:, 6, 8:8 + B].unsqueeze(2).broadcast_to([P, B, GB_]),
                                    1.0, None, ALU.add).then_inc(set_cols, 1)
                dve.wait_ge(set_khi, i + 1)
                split_mix(1, i, "lo").then_inc(set_mix, 1)
                if i == 0:
                    split_hi(0)
            dve.wait_ge(p_wv, 1)
            v.tensor_copy(wvT[:, :], ps[:, 4, 0:P]).then_inc(set_wv, 1)
            dve.wait_ge(set_silu, 1)
            v.tensor_copy(silu_bc[:, :, :], siluT[:, :].unsqueeze(2).broadcast_to([P, B, P])).then_inc(set_silu, 1)
            v.tensor_copy(carry[:, :], region0[:, :]).then_inc(s_cr, 1)
            v.tensor_copy(vbd[:, :, :, :, HD:VW].rearrange("p t h c o -> p (t h) (c o)"),
                          blk_mask[:, :, 0].unsqueeze(1).broadcast_to([P, TG * H, NC])).then_inc(c_dve, 1)

            def setup_rows(b):
                dve.wait_ge(p_rows, b + 1)
                v.tensor_copy(mod_bc[:, b, :, :].rearrange("p j d -> p (j d)"), m_ps).then_inc(set_rows, 1)

            def setup_norms():
                dve.wait_ge(l_gate, 64)
                v.tensor_copy(wo_perm[:, :].rearrange("p (q s d) -> p s q d", q=HH, s=2),
                              wo_sb[:, :].rearrange("p (s q d) -> p s q d", q=HH, s=2)).then_inc(set_perm, 1)
                v.tensor_tensor(wg_sq[:, :], wg_sb[:, :], wg_sb[:, :], ALU.mult).then_inc(c_wg, 1)
                dve.wait_ge(c_wg, 1)
                v.tensor_reduce(wg_n[:, 0:1], wg_sq[:, :], AX.X, ALU.add).then_inc(c_wg, 1)
                dve.wait_ge(c_wg, 2)
                v.tensor_scalar(wg_n[:, 1:2], wg_n[:, 0:1], 1e-8, None, ALU.max).then_inc(c_wg, 1)

            def setup_wg():
                dve.wait_ge(c_wgr, 1)
                v.tensor_scalar(wg_u[:, :], wg_sb[:, :], wg_n[:, 2:3], None, ALU.mult).then_inc(set_wg, 1)

            rows = mod_bc[:, :, 0:4:3, :]

            def setup_mod_a():
                dve.wait_ge(set_rows, B)
                v.tensor_scalar(signs[:, :, :, :], rows, 0.0, 2.0, ALU.is_ge, ALU.mult)
                for j in range(2):
                    last = v.scalar_tensor_tensor(out=mags[:, :, j, :], in0=rows[:, :, j, :], scalar=-1.0, in1=rows[:, :, j, :],
                                                  op0=ALU.mult, op1=ALU.max)
                last.then_inc(c_mod, 1)

            def setup_mod_b():
                v.tensor_scalar(mod_bc[:, :, 2, :], mod_bc[:, :, 2, :], 1.0, None, ALU.add)
                dve.wait_ge(c_mod, 1)
                v.tensor_scalar(mags[:, :, :, :], mags[:, :, :, :], 0.25, None, ALU.max).then_inc(c_mod, 1)
                dve.wait_ge(c_mod, 2)
                for j in range(2):
                    last = v.scalar_tensor_tensor(out=rows[:, :, j, :], in0=signs[:, :, j, :], scalar=-1.0, in1=mags[:, :, j, :],
                                                  op0=ALU.add, op1=ALU.mult)
                last.then_inc(set_mod, 1)

            def setup_turns():
                dve.wait_ge(p_turn, 1)
                v.tensor_copy(woT[:, :], ps[:, 6, 0:P])
                v.tensor_copy(wredT[:, :], ps[0:GD, 6, P:2 * P])
                v.tensor_copy(wgT[:, :], ps[0:GD, 6, 2 * P:2 * P + E]).then_inc(set_turn, 1)

            def setup_gate():
                dve.wait_ge(p_gate, 1)
                v.tensor_copy(w_gate[:, :], ps[:, 6, 0:E]).then_inc(set_gate, 1)

            def features(g, h):
                if not (isinstance(g, int) and g == 0 and h < 4):
                    dve.wait_ge(s_a, H * g + h - 3)
                for j in range(2):
                    dve.wait_ge(s_exp, 2 * (H * g + h) + j + 1)
                    v.scalar_tensor_tensor(out=phi[:, h % 4, j, :], in0=x_ps[h % 2][:, j, :], scalar=0.0,
                                           in1=ebuf[:, h % 2, j, :], op0=ALU.max, op1=ALU.add).then_inc(s_phi, 1)

            def keep_values(g, c, first):
                dve.wait_ge(s_vs, g + 1)
                if not first:
                    dve.wait_ge(s_av, 2 * g)
                last = v.tensor_scalar(vbd[:, :, :, c, 0:HD].rearrange("p t h d -> p (t h) d"),
                                       vals[:, :, :, :].rearrange("p t h d -> p (t h) d"),
                                       blk_mask[:, c, 0:1], None, ALU.mult)
                if c == NC - 1:
                    last.then_inc(s_vbd, 1)

            o3 = o_ps.rearrange("p (u w) -> p u w", w=VW)

            def normalise_sum(g, half):
                dve.wait_ge(s_av, 2 * g + half + 1)
                v.tensor_scalar(den[:, :], o3[:, :, HD], 1e-8, None, ALU.add).then_inc(s_nrm, 1)

            def normalise_inverse(g, half):
                dve.wait_ge(s_nrm, 2 * (2 * g + half) + 1)
                v.reciprocal(rden[:, :], den[:, :]).then_inc(s_nrm, 1)

            def normalise_out(g, half):
                dve.wait_ge(s_nrm, 2 * (2 * g + half) + 2)
                v.tensor_tensor(o_sb[:, :, half, :], o3[:, :, 0:HD], rden[:, :].unsqueeze(2).broadcast_to([P, TG * NC, HD]),
                                ALU.mult).then_inc(s_on, 1)

            def turn_o(g, first):
                dve.wait_ge(s_on, 2 * g + 2)
                if not first:
                    dve.wait_ge(s_y, g)
                v.transpose(oT[:, :, :].rearrange("p t s -> p (t s)"), o_sb[:, :, :, :].rearrange("p u s d -> p (u s d)")).then_inc(s_ot, 1)

            def residual(g):
                dve.wait_ge(s_y, g + 1)
                dve.wait_ge(s_xb, g + 1)
                if not (isinstance(g, int) and g == 0) and not is_last(g):
                    dve.wait_ge(s_rec, 32 * g)
                v.tensor_tensor(x2_of(g), (t_ps if is_last(g) else m_ps).rearrange("p (t d) -> p t d", t=TG), xb[:, :, :], ALU.add).then_inc(s_x2, 1)

            def norm2_stats(g):
                dve.wait_ge(s_x2, g + 1)
                for t in range(TG):
                    last = v.bn_stats(ln2_st[:, t, :], x2_of(g)[:, t, :])
                last.then_inc(s_ln2, 1)

            def norm2_moments(g):
                dve.wait_ge(s_ln2, 3 * g + 1)
                dve.sem_inc(seq_dve, 1)
                for t in range(TG):
                    last = v.bn_aggr(ln2_mv[:, t, :], ln2_st[:, t, :])
                last.then_inc(s_ln2, 1)
                dve.wait_ge(s_ln2, 3 * g + 2)
                v.tensor_scalar(ln2_ve[:, :], ln2_mv[:, :, 1], EPS, None, ALU.add).then_inc(s_ln2, 1)

            def norm2_center(g, tiles, first):
                if not first:
                    dve.wait_ge(s_h2, g)
                for t in tiles:
                    last = v.scalar_tensor_tensor(out=h2[:, t, :], in0=x2_of(g)[:, t, :], scalar=ln2_mv[:, t, 0:1],
                                                  in1=mod_bc[:, bass.ds(g // GB_, 1), 2, :].rearrange("p a d -> p (a d)"),
                                                  op0=ALU.subtract, op1=ALU.mult)
                if TG - 1 in tiles:
                    last.then_inc(s_nh, 1)

            def norm2_scale_last():
                dve.wait_ge(s_rs2, NG)
                dve.wait_ge(s_nh, NG)
                v.tensor_tensor(h2[:, :, :], h2[:, :, :], ln2_rs[:, :].unsqueeze(2).broadcast_to([P, TG, D]), ALU.mult).then_inc(s_nm, 1)
                dve.wait_ge(s_nm, NG)
                v.tensor_tensor(h2m_of(NG - 1), h2[:, :, :], mod_bc[:, B - 1:B, 1, :].broadcast_to([P, TG, D]),
                                ALU.add).then_inc(s_h2, 1)

            def route_max(g):
                dve.wait_ge(s_lgs, g + 1)
                v.tensor_reduce(top[:, :], lg_sb[:, :, :], AX.X, ALU.max).then_inc(s_rt, 1)

            def route_below(g):
                dve.wait_ge(s_rt, 3 * g + 1)
                v.tensor_tensor(lgd[:, :, :], lg_sb[:, :, :], top[:, :].unsqueeze(2).broadcast_to([P, TG, E]), ALU.subtract).then_inc(s_lgd, 1)

            def route_first(g):
                dve.wait_ge(s_lgd, g + 1)
                v.scalar_tensor_tensor(out=cand[:, :, :], in0=lgd[:, :, :], scalar=0.0,
                                       in1=rev[:, :].unsqueeze(1).broadcast_to([P, TG, E]), op0=ALU.is_ge, op1=ALU.mult).then_inc(s_rt, 1)
                dve.wait_ge(s_rt, 3 * g + 2)
                v.tensor_reduce(cmax[:, :], cand[:, :, :], AX.X, ALU.max).then_inc(s_rt, 1)
                dve.wait_ge(s_rt, 3 * g + 3)
                v.tensor_tensor(pick[:, :, :], cand[:, :, :], cmax[:, :].unsqueeze(2).broadcast_to([P, TG, E]),
                                ALU.is_equal).then_inc(s_pick, 1)

            def score_sum(g):
                dve.wait_ge(s_ex, g + 1)
                v.tensor_reduce(lgs[:, :], lge[:, :, :], AX.X, ALU.add).then_inc(s_gs, 1)

            def score_inverse(g, first):
                dve.wait_ge(s_gs, g + 1)
                if not first:
                    dve.wait_ge(s_gbs, g)
                v.reciprocal(score[:, :], lgs[:, :]).then_inc(s_sc, 1)

            def position_rows(g):
                dve.wait_ge(s_rk, g + 1)
                dve.wait_ge(s_cr, g + 1)
                v.tensor_tensor(posf[:, :, :], m_ps[:, 0:TG * E].rearrange("p (t e) -> p t e", e=E),
                                carry[:, :].unsqueeze(1).broadcast_to([P, TG, E]), ALU.add).then_inc(s_ps, 1)

            def position_own(g):
                dve.wait_ge(s_ps, 2 * g + 1)
                v.tensor_tensor(carry[:, :], m_ps[:, TG * E:(TG + 1) * E], carry[:, :], ALU.add).then_inc(s_cr, 1)
                v.tensor_tensor(posr3[:, :, :], posf[:, :, :], pick[:, :, :], ALU.mult).then_inc(s_ps, 1)

            def position_sum(g):
                dve.wait_ge(s_ps, 2 * g + 2)
                v.tensor_reduce(posr[:, :], posr3[:, :, :], AX.X, ALU.add).then_inc(s_pr, 1)

            def position_out(g, first):
                dve.wait_ge(s_pr, g + 1)
                if not first and not is_last(g):
                    dve.wait_ge(s_scat, 16 * TG * g)
                v.tensor_copy((pos_last if is_last(g) else pos)[:, :], posr[:, :]).then_inc(s_pos, 1)

            def step(g, prev, prev2, nxt, first=False, firstp=False, firstp2=False):
                for h in range(H):
                    features(g, h)
                    if isinstance(g, int) and g == 0:
                        if h == 0:
                            setup_norms()
                        if h < B:
                            setup_rows(h)
                        if h == 3:
                            setup_wg()
                        if h == 4:
                            setup_mod_a()
                        if h == 6:
                            setup_turns()
                            setup_mod_b()
                        if h == 7:
                            setup_gate()
                    if h == 0:
                        if prev:
                            normalise_sum(g - 1, 0)
                        if nxt:
                            norm1_stats(g + 1, range(TG // 2), False)
                        if prev:
                            normalise_inverse(g - 1, 0)
                        if nxt:
                            norm1_stats(g + 1, range(TG // 2, TG), False)
                        if prev:
                            normalise_out(g - 1, 0)
                    if h == 2:
                        if prev:
                            normalise_sum(g - 1, 1)
                        if nxt:
                            norm1_moments(g + 1)
                        if prev:
                            normalise_inverse(g - 1, 1)
                        if nxt:
                            norm1_variance(g + 1)
                        if prev:
                            normalise_out(g - 1, 1)
                            turn_o(g - 1, firstp)
                    if h == 3:
                        keep_values(g, 0, first)
                        keep_values(g, 1, first)
                    if h == 4:
                        if prev2:
                            route_max(g - 2)
                        keep_values(g, 2, first)
                        if prev2:
                            route_below(g - 2)
                        keep_values(g, 3, first)
                        if prev2:
                            route_first(g - 2)
                    if h == 5 and prev:
                        residual(g - 1)
                    if h == 5 and nxt:
                        split_hi(g + 1)
                    if h == 6:
                        if prev2:
                            score_sum(g - 2)
                        if prev:
                            norm2_stats(g - 1)
                        if prev2:
                            score_inverse(g - 2, firstp2)
                        if prev:
                            norm2_moments(g - 1)
                    if h == 7:
                        if prev2:
                            position_rows(g - 2)
                        if prev:
                            norm2_center(g - 1, range(0, 1), firstp)
                        if prev2:
                            position_own(g - 2)
                        if prev:
                            norm2_center(g - 1, range(1, 2), firstp)
                        if prev2:
                            position_sum(g - 2)
                        if prev:
                            norm2_center(g - 1, range(2, TG), firstp)
                        if prev2:
                            position_out(g - 2, firstp2)

            step(0, False, False, True, first=True)
            step(1, True, False, True, firstp=True)
            step(2, True, True, True, firstp2=True)
            with dve.Fori(3, NG - 1) as g:
                step(g, True, True, True)
            step(NG - 1, True, True, False)

            for half in range(2):
                normalise_sum(NG - 1, half)
                normalise_inverse(NG - 1, half)
                normalise_out(NG - 1, half)
            turn_o(NG - 1, False)
            residual(NG - 1)
            norm2_stats(NG - 1)
            route_max(NG - 2)
            norm2_moments(NG - 1)
            route_below(NG - 2)
            route_first(NG - 2)
            norm2_center(NG - 1, range(TG // 2), False)
            score_sum(NG - 2)
            norm2_center(NG - 1, range(TG // 2, TG), False)
            score_inverse(NG - 2, False)
            position_rows(NG - 2)
            position_own(NG - 2)
            position_sum(NG - 2)
            position_out(NG - 2, False)
            norm2_scale_last()
            route_max(NG - 1)
            route_below(NG - 1)
            route_first(NG - 1)
            score_sum(NG - 1)
            position_rows(NG - 1)
            score_inverse(NG - 1, False)
            position_own(NG - 1)
            position_sum(NG - 1)
            v.tensor_copy(carry_i[:, :], carry[:, :]).then_inc(s_table, 1)
            position_out(NG - 1, False)

            v.tensor_tensor(cnt[:, :], carry[:, :], region0[:, :], ALU.subtract).then_inc(s_tab, 1)
            dve.wait_ge(s_tab, 1)
            v.tensor_tensor(full[:, :, :], cnt[:, :].unsqueeze(2).broadcast_to([P, E, NT]),
                            tiles128[:, :].unsqueeze(1).broadcast_to([P, E, NT]), ALU.is_gt).then_inc(s_tab, 1)
            dve.wait_ge(s_tab, 2)
            v.tensor_reduce(nt[:, :], full[:, :, :], AX.X, ALU.add).then_inc(s_tab, 1)
            dve.wait_ge(s_tab, 3)
            v.tensor_scalar(skip[:, :], nt[:, :], -float(P), float(REGION), ALU.mult, ALU.add)
            v.tensor_copy(endt[:, 0, :], nt[:, :]).then_inc(s_tab, 1)
            src, n = 0, 4
            for sh in (1, 2, 4):
                dve.wait_ge(s_tab, n)
                v.tensor_copy(endt[:, 1 - src, 0:sh], endt[:, src, 0:sh])
                v.tensor_tensor(endt[:, 1 - src, sh:E], endt[:, src, sh:E], endt[:, src, 0:E - sh], ALU.add).then_inc(s_tab, 1)
                src, n = 1 - src, n + 1
            dve.wait_ge(s_tab, 7)
            v.tensor_tensor(past[:, :, :], slot_no[:, :].unsqueeze(2).broadcast_to([P, SLOTS, E]),
                            endt[:, src, :].unsqueeze(1).broadcast_to([P, SLOTS, E]), ALU.is_ge).then_inc(s_tab, 1)
            dve.wait_ge(s_tab, 8)
            v.tensor_tensor(hop[:, :, :], past[:, :, :], skip[:, :].unsqueeze(1).broadcast_to([P, SLOTS, E]), ALU.mult)
            v.tensor_reduce(expf[:, 0, :], past[:, :, :], AX.X, ALU.add).then_inc(s_tab, 1)
            dve.wait_ge(s_tab, 9)
            v.tensor_scalar(exp_i[:, :], expf[:, 0, :], float(E - 1), None, ALU.min)
            v.tensor_reduce(rowf[:, 0, :], hop[:, :, :], AX.X, ALU.add).then_inc(s_tab, 1)
            dve.wait_ge(s_tab, 10)
            v.scalar_tensor_tensor(out=rowf[:, 1, :], in0=slot_no[:, :], scalar=float(P), in1=rowf[:, 0, :],
                                   op0=ALU.mult, op1=ALU.add).then_inc(s_tab, 1)
            dve.wait_ge(s_tab, 11)
            v.tensor_scalar(row_i[:, :], rowf[:, 1, :], float(DUMMY), None, ALU.min).then_inc(s_table, 1)
            dve.wait_ge(s_table, 2)

            def expert_of(s):
                return dve.value_load(exp_i[0:1, bass.ds(s, 1)], min_val=0, max_val=E - 1)

            def take_weights(s, b):
                e = dve.value_load(exp_i[0:1, bass.ds(s, 1)], min_val=0, max_val=E - 1)
                v.tensor_copy(w_slot[b], w1b2[:, bass.ds(e * (F + D), F + D)]).then_inc(f_w, 1)

            def finish(s, b, k):
                dve.wait_ge(f_w, s + 1)
                dve.wait_ge(f_y, s + 1)
                v.tensor_tensor(y1[:, b % 2, :], ps[:, 6 + b % 2, 0:D], w_slot[b][:, F:F + D], ALU.add).then_inc(f_s, 1)
                if not (isinstance(s, int) and s < RING):
                    dve.wait_ge(f_out[b], 16 * k)
                v.tensor_copy(tok[:, b:b + 1], rin[:, b, 3 * D:R])
                dve.wait_ge(f_s, 2 * s + 1)
                v.tensor_tensor(y2[:, b % 2, :], y1[:, b % 2, :], rin[:, b, 2 * D:3 * D], ALU.mult).then_inc(f_s, 1)
                dve.wait_ge(f_s, 2 * s + 2)
                v.tensor_tensor(yo[:, b, :], y2[:, b % 2, :], rin[:, b, D:2 * D], ALU.add).then_inc(f_yd, 1)

            dve.wait_ge(l_exp, 64)
            for s in range(3):
                take_weights(s, s)

            def run(s, b):
                take_weights(s + 1, (b + 1) % RING)
                finish(s - 2, (b - 2) % RING, (s - 2) // RING)

            begin = RING + 2
            end = begin + (SLOTS - 1 - begin) // RING * RING
            for s in range(2, begin):
                run(s, s % RING)
            with dve.Fori(begin, end - RING + 1, RING) as s:
                for d in range(RING):
                    run(s + d, (begin + d) % RING)
            for s in range(end, SLOTS - 1):
                run(s, s % RING)
            for s in range(SLOTS - 3, SLOTS):
                finish(s, s % RING, s // RING)


_INS = ["L0_attn_x", "L0_attn_w_qkv", "L0_attn_w_out", "L0_attn_b_out", "L0_attn_proj", "L0_ffn_w_red", "L0_ffn_wg",
        "L0_ffn_w1", "L0_ffn_b1", "L0_ffn_w2", "L0_ffn_b2", "L0_c", "L0_wmod"]


def kernel(**inputs):
    import numpy as np
    import concourse.bacc as bacc
    from concourse.bass_utils import run_bass_kernel_spmd

    nc = bacc.Bacc("TRN2", target_bir_lowering=False, num_devices=1)
    arrays, args = {}, []
    for name in _INS:
        a = np.ascontiguousarray(inputs[name])
        if name == "L0_c":
            a = np.ascontiguousarray(a.T)
        if name == "L0_ffn_b1":
            a = np.ascontiguousarray(a.reshape(a.shape[0], -1, P).transpose(2, 0, 1).reshape(P, -1))
        arrays[f"in_{name}"] = a
        args.append(nc.dram_tensor(f"in_{name}", a.shape, mybir.dt.from_np(a.dtype), kind="ExternalInput").ap())
    shape = inputs["L0_attn_x"].shape
    out = nc.dram_tensor("out_0", shape, F32, kind="ExternalOutput").ap()
    adaln_kernel(nc, *args, out)
    r = run_bass_kernel_spmd(nc, [arrays], core_ids=[0])
    return r.results[0]["out_0"]
```
